# Optimizing a Trainium2 kernel written in Bass

```python
import numpy as np
import jax
import jax.numpy as jnp

def _softmax(x, axis=-1):
    return jax.nn.softmax(x, axis=axis)

def _gelu(x):
    return jax.nn.gelu(x, approximate=True)

def _silu(x):
    return jax.nn.silu(x)

def _sigmoid(x):
    return jax.nn.sigmoid(x)

def _layernorm(x, axis=-1, eps=1e-05):
    m = jnp.mean(x, axis=axis, keepdims=True)
    v = jnp.var(x, axis=axis, keepdims=True)
    return (x - m) / jnp.sqrt(v + eps)

def _scatter_add(tgt, idx, src, axis=0):
    return tgt.at[idx].add(src)

def _segment_sum(src, seg, n):
    return jax.ops.segment_sum(src, seg, n)
kernel_name = 'mk_flamingo_gated_d1_seqx_r8_d55453'

def setup_inputs(seed: int=0):
    np.random.seed(seed)
    _w = jnp.asarray

    def _rec_inputs():
        import jax
        import jax.numpy as jnp
        _rk = jax.random.key(seed)
        x = 7.22e-05 + 1 * jax.random.normal(jax.random.fold_in(_rk, 1), (8, 128, 512), jnp.float32)
        _lenS = 128 - jax.random.randint(jax.random.fold_in(_rk, 7), (8,), 0, max(1, 128 // 4) + 1, jnp.int32)
        _lenS2 = 128 - jax.random.randint(jax.random.fold_in(_rk, 8), (8,), 0, max(1, 128 // 4) + 1, jnp.int32)
        _ctx_4096P = jax.random.normal(jax.random.fold_in(_rk, 11), (8, 16, 512), jnp.float32)
        _ctx_4096c = jax.random.dirichlet(jax.random.fold_in(_rk, 511), 0.3 * jnp.ones((16,), jnp.float32), (8, 128))
        _ctx_4096t = jnp.einsum('bsk,bkd->bsd', _ctx_4096c, _ctx_4096P)
        _ctx_4096t = _ctx_4096t * jax.lax.rsqrt(jnp.mean(jnp.square(_ctx_4096t)) + 1e-12) * 0.953939
        ctx_4096 = 4.13588e-05 + 0.999923 * (_ctx_4096t + 0.3 * jax.random.normal(jax.random.fold_in(_rk, 611), (8, 128, 512), jnp.float32))
        _validS = jnp.arange(128)[None, :] < _lenS[:, None]
        _validS2 = jnp.arange(128)[None, :] < _lenS2[:, None]
        _causal = jnp.tril(jnp.ones((128, 128), dtype=bool))
        mask_BxSxS2_bk0 = jnp.logical_not(jnp.broadcast_to(_validS2[:, None, :], (8, 128, 128)))
        _g = jax.random.normal(jax.random.fold_in(_rk, 9001), (2, 1), jnp.float32)
        _g = jnp.sign(_g) * jnp.maximum(jnp.abs(_g), 1.0) + (_g == 0) * 1.0
        g_xattn = _g[0]
        g_ffn = _g[1]
        return (x, ctx_4096, mask_BxSxS2_bk0, g_xattn, g_ffn)
    x, ctx_4096, mask_BxSxS2_bk0, g_xattn, g_ffn = _rec_inputs()

    def _L0_xattn_setup():
        import jax, jax.numpy as jnp
        import numpy as np
        B, LQ, LK, D, H, DH = (2, 128, 128, 512, 32, 128)
        EPS = 1e-05

        def _rmsnorm(x, weight):
            var = jnp.mean(jnp.square(x), axis=-1, keepdims=True)
            return x * jax.lax.rsqrt(var + EPS) * weight
        key = jax.random.key(seed)
        ks = jax.random.split(key, 8)
        scale = 0.02
        return {'hidden_states': jax.random.normal(ks[0], (B, LQ, D), jnp.float32), 'key_value_states': jax.random.normal(ks[1], (B, LK, D), jnp.float32), 'attention_mask': jax.random.randint(ks[2], (B, LQ, LK), 0, 2) > 0, 'position_bias': jax.random.normal(ks[3], (H, LQ, LK), jnp.float32), 'ln_weight': jnp.ones((D,), jnp.float32), 'w_q': jax.random.normal(ks[4], (H * DH, D), jnp.float32) * scale, 'w_k': jax.random.normal(ks[5], (H * DH, D), jnp.float32) * scale, 'w_v': jax.random.normal(ks[6], (H * DH, D), jnp.float32) * scale, 'w_out': jax.random.normal(ks[7], (D, H * DH), jnp.float32) * scale}
    _L0_xattn_all = _L0_xattn_setup()
    _L0_xattn_in = {k: v for k, v in _L0_xattn_all.items() if k in ('position_bias', 'ln_weight', 'w_q', 'w_k', 'w_v', 'w_out')}
    del _L0_xattn_all

    def _L0_ffn_setup():
        import jax, jax.numpy as jnp
        import numpy as np
        SCALING = 32.0 / 16.0
        key = jax.random.key(seed)
        ks = jax.random.split(key, 7)
        B, T, D, O, R, E = (4, 256, 512, 512, 16, 8)
        x = jax.random.normal(ks[0], (B, T, D), dtype=jnp.float32)
        base_W = jax.random.normal(ks[1], (O, D), dtype=jnp.float32) * D ** (-0.5)
        base_b = jax.random.normal(ks[2], (O,), dtype=jnp.float32) * 0.01
        router_W = jax.random.normal(ks[3], (2 * E - 1, D), dtype=jnp.float32) * D ** (-0.5)
        router_b = jax.random.normal(ks[4], (2 * E - 1,), dtype=jnp.float32) * 0.01
        A = jax.random.normal(ks[5], (E, R, D), dtype=jnp.float32) * D ** (-0.5)
        Bm = jax.random.normal(ks[6], (E, O, R), dtype=jnp.float32) * R ** (-0.5)
        assigned_idx = 0
        others = [i for i in range(E) if i != assigned_idx]
        expert_map = jnp.array([assigned_idx] * E + others, dtype=jnp.int32)
        return {'x': x, 'base_W': base_W, 'base_b': base_b, 'router_W': router_W, 'router_b': router_b, 'A': A, 'B': Bm, 'expert_map': expert_map}
    _L0_ffn_all = _L0_ffn_setup()
    _L0_ffn_in = {k: v for k, v in _L0_ffn_all.items() if k in ('base_W', 'base_b', 'router_W', 'router_b', 'A', 'B', 'expert_map')}
    del _L0_ffn_all
    return {'x': x, 'ctx_4096': ctx_4096, 'mask_BxSxS2_bk0': mask_BxSxS2_bk0, 'g_xattn': g_xattn, 'g_ffn': g_ffn, 'L0_xattn_position_bias': _L0_xattn_in['position_bias'], 'L0_xattn_ln_weight': _L0_xattn_in['ln_weight'], 'L0_xattn_w_q': _L0_xattn_in['w_q'], 'L0_xattn_w_k': _L0_xattn_in['w_k'], 'L0_xattn_w_v': _L0_xattn_in['w_v'], 'L0_xattn_w_out': _L0_xattn_in['w_out'], 'L0_ffn_base_W': _L0_ffn_in['base_W'], 'L0_ffn_base_b': _L0_ffn_in['base_b'], 'L0_ffn_router_W': _L0_ffn_in['router_W'], 'L0_ffn_router_b': _L0_ffn_in['router_b'], 'L0_ffn_A': _L0_ffn_in['A'], 'L0_ffn_B': _L0_ffn_in['B'], 'L0_ffn_expert_map': _L0_ffn_in['expert_map']}

def reference(x, ctx_4096, mask_BxSxS2_bk0, g_xattn, g_ffn, L0_xattn_position_bias, L0_xattn_ln_weight, L0_xattn_w_q, L0_xattn_w_k, L0_xattn_w_v, L0_xattn_w_out, L0_ffn_base_W, L0_ffn_base_b, L0_ffn_router_W, L0_ffn_router_b, L0_ffn_A, L0_ffn_B, L0_ffn_expert_map):
    import jax
    import jax.numpy as jnp

    def _L0_xattn_ref(hidden_states, key_value_states, attention_mask, position_bias, ln_weight, w_q, w_k, w_v, w_out):
        import jax, jax.numpy as jnp
        import numpy as np
        B, LQ, LK, D, H, DH = (2, 128, 128, 512, 32, 128)
        EPS = 1e-05

        def _rmsnorm(x, weight):
            var = jnp.mean(jnp.square(x), axis=-1, keepdims=True)
            return x * jax.lax.rsqrt(var + EPS) * weight
        x = _rmsnorm(hidden_states, ln_weight)
        b, lq, _ = x.shape
        lk = key_value_states.shape[1]
        h_q = (x @ w_q.T).reshape(b, lq, H, DH)
        h_k = (key_value_states @ w_k.T).reshape(b, lk, H, DH)
        h_v = (key_value_states @ w_v.T).reshape(b, lk, H, DH)
        score = jnp.einsum('bqhd,bkhd->bhqk', h_q, h_k)
        score = score + position_bias[None]
        m = attention_mask[:, None]
        score = jnp.where(m, score, -jnp.inf)
        score = jax.nn.softmax(score, axis=-1)
        score = jnp.where(m, score, 0.0)
        attn = jnp.einsum('bhqk,bkhd->bqhd', score, h_v).reshape(b, lq, H * DH)
        out = attn @ w_out.T
        return hidden_states + out

    def _L0_ffn_ref(x, base_W, base_b, router_W, router_b, A, B, expert_map):
        import jax, jax.numpy as jnp
        import numpy as np
        SCALING = 32.0 / 16.0
        E = A.shape[0]
        base_out = jnp.einsum('btd,od->bto', x, base_W) + base_b
        logits = jnp.einsum('btd,nd->btn', x, router_W) + router_b
        probs = jax.nn.softmax(logits, axis=-1)
        topk_p, topk_i = jax.lax.top_k(probs, E)
        mapped = expert_map[topk_i]
        onehot = (mapped[..., None] == jnp.arange(E)).astype(x.dtype)
        w = jnp.einsum('btk,btke->bte', topk_p, onehot)
        h = jnp.einsum('btd,erd->bter', x, A)
        lora = jnp.einsum('bter,eor->bto', h * w[..., None], B) * SCALING
        return base_out + lora
    x = x + jnp.tanh(g_xattn[0]) * _L0_xattn_ref(_layernorm(x, axis=-1), ctx_4096, mask_BxSxS2_bk0, L0_xattn_position_bias, L0_xattn_ln_weight, L0_xattn_w_q, L0_xattn_w_k, L0_xattn_w_v, L0_xattn_w_out)
    x = x + jnp.tanh(g_ffn[0]) * _L0_ffn_ref(_layernorm(x, axis=-1), L0_ffn_base_W, L0_ffn_base_b, L0_ffn_router_W, L0_ffn_router_b, L0_ffn_A, L0_ffn_B, L0_ffn_expert_map)
    return x

_drawn_inputs = setup_inputs


def setup_inputs(seed=0):
    import zlib

    import numpy as np

    out = dict(_drawn_inputs(seed))
    spreads = {'L0_xattn_ln_weight': (1.0, 0.2)}
    factors = {'L0_ffn_base_b': 8.0, 'L0_ffn_router_b': 8.0}
    for name, (base, spread) in spreads.items():
        noise = np.random.default_rng([zlib.crc32(name.encode()), seed]).standard_normal(out[name].shape)
        drawn = base * np.exp(spread * noise) if base else spread * noise
        out[name] = jnp.asarray(drawn.astype(out[name].dtype))
    for name, factor in factors.items():
        out[name] = (out[name] * factor).astype(out[name].dtype)
    return out
```

```python
from contextlib import ExitStack

import concourse.bass as bass
from concourse import mybir

F32 = mybir.dt.float32
F32R = mybir.dt.float32r
U8 = mybir.dt.uint8
I32 = mybir.dt.int32
ALU = mybir.AluOpType
ACT = mybir.ActivationFunctionType
AX = mybir.AxisListType

P = 128
B, S, D = 8, 128, 512
H, DH = 32, 128
DC = D // P
HALVES = 2
BH = B // HALVES
TH = BH * S
G = H // 2
UNITS = 4 * G
NR, E, R = 15, 8, 16
ER = E * R
RW = ER + 16
LN_EPS = 1e-5
RMS_EPS = 1e-5
LORA_SCALE = 2.0
MASKED = 2.0 ** 100


def build(nc, x, ctxT, mask, g_xattn, g_ffn, bias, lnw, wqk, wv, wo, baseT, base_b, loraR, router_b,
          lora_B, expert_map, out):
    with ExitStack() as ctx:
        def sb(name, shape, dt=F32):
            return ctx.enter_context(nc.sbuf_tensor(name, shape, dt))

        def psum(name, shape):
            return ctx.enter_context(nc.psum_tensor(name, shape, F32))

        def sem(name):
            return ctx.enter_context(nc.semaphore(name))

        xT_hi, xT_lo = sb("xT_hi", [P, DC, B * S], F32R), sb("xT_lo", [P, DC, B * S], F32R)
        cT_hi, cT_lo = sb("cT_hi", [P, DC, B * S], F32R), sb("cT_lo", [P, DC, B * S], F32R)
        acc = sb("acc", [P, B, D])
        qk_raw = sb("qk_raw", [P, 2, 2, DC, DH])
        qk_hi, qk_lo = sb("qk_hi", [P, 2, 2, DC, DH], F32R), sb("qk_lo", [P, 2, 2, DC, DH], F32R)
        v_raw = sb("v_raw", [P, DC, 2 * DH])
        v_hi, v_lo = sb("v_hi", [P, DC, 2 * DH], F32R), sb("v_lo", [P, DC, 2 * DH], F32R)
        o_raw = sb("o_raw", [P, 2, D])
        o_hi, o_lo = sb("o_hi", [P, 2, D], F32R), sb("o_lo", [P, 2, D], F32R)
        V_hi, V_lo = sb("V_hi", [P, B, 2 * DH], F32R), sb("V_lo", [P, B, 2 * DH], F32R)
        A_hi, A_lo = sb("A_hi", [P, HALVES, 2, TH], F32R), sb("A_lo", [P, HALVES, 2, TH], F32R)
        Q_hi, Q_lo = sb("Q_hi", [P, TH], F32R), sb("Q_lo", [P, TH], F32R)
        K_hl = sb("K_hl", [P, BH, 2, S], F32R)
        P_hl = sb("P_hl", [P, BH, 2, S], F32R)
        bias_sb = sb("bias_sb", [P, 2, S])
        maskneg = sb("maskneg", [P, B, S])
        bm = sb("bm", [P, BH, S])
        bms = sb("bms", [P, BH, S])
        small_s = sb("small_s", [P, BH, S])
        s_sb = sb("s_sb", [P, BH, S])
        p_exp = sb("p_exp", [P, BH, S])
        p_norm = sb("p_norm", [P, BH, S])
        small_a = sb("small_a", [P, TH])
        a_rest = sb("a_rest", [P, TH])
        stage = sb("stage", [P, DC, D])
        row_bc = sb("row_bc", [P, D])
        ident = sb("ident", [P, P])
        valid = sb("valid", [P, B])
        negmax, rowsum = sb("negmax", [P, BH]), sb("rowsum", [P, BH])
        rinv, rscale = sb("rinv", [P, BH]), sb("rscale", [P, BH])
        gate = sb("gate", [P, 2])
        tgate = sb("tgate", [P, 2])
        half_neg = sb("half_neg", [P, BH])
        bn6 = sb("bn6", [P, 2, BH, 6])
        mv = sb("mv", [P, 2, BH, 2])
        rstd_in, rstd = sb("rstd_in", [P, 2, BH]), sb("rstd", [P, 2, BH])
        rms_in, rms_r = sb("rms_in", [P, 2, BH]), sb("rms_r", [P, 2, BH])
        mask8 = p_norm.ap().rearrange("p a b -> p (a b)")[:, 0:B * S // 4].bitcast(U8)
        mask8 = mask8.rearrange("p (b k) -> p b k", b=B)
        rb_bc = sb("rb_bc", [P, NR])
        emap = sb("emap", [P, NR], I32)
        emap_f = sb("emap_f", [P, NR])
        eidx = sb("eidx", [P, E], I32)
        eidx_f = sb("eidx_f", [P, E])
        onehot = sb("onehot", [P, E, NR])
        lg = sb("lg", [P, BH, NR])
        lmax, lsum, lrec = sb("lmax", [P, BH]), sb("lsum", [P, BH]), sb("lrec", [P, BH])
        le, probs = sb("le", [P, BH, NR]), sb("probs", [P, BH, NR])
        top8 = sb("top8", [P, BH, 8])
        rest = sb("rest", [P, BH, NR])
        chosen = sb("chosen", [P, BH, NR])
        picked = small_s.ap().rearrange("p a b -> p (a b)")[:, 0:BH * E * NR]
        picked = picked.rearrange("p (i e n) -> p i e n", i=BH, e=E)
        we = sb("we", [P, BH, E])

        QP = psum("QP", [P, TH])
        Kb = psum("Kb", [P, TH])
        Vb = psum("Vb", [P, 2, 2 * DH])
        Ob = psum("Ob", [P, D])
        Sb = psum("Sb", [P, BH, 2, S])
        Ab = psum("Ab", [P, BH, 2, S])

        ld_c, ld_x, ld_o = sem("ld_c"), [sem("ld_xA"), sem("ld_xB")], sem("ld_o")
        ld_cB = sem("ld_cB")
        ld_wv = sem("ld_wv")
        ld_qk = [sem("ld_qk0"), sem("ld_qk1")]
        ld_bias = [sem("ld_bias0"), sem("ld_bias1")]
        ld_lnw, ld_mask, ld_gate = sem("ld_lnw"), sem("ld_mask"), sem("ld_gate")
        ld_small, ld_base, ld_lora, ld_loraB = sem("ld_small"), sem("ld_base"), sem("ld_lora"), sem("ld_loraB")
        ld_x2 = [sem("ld_x2A"), sem("ld_x2B")]
        ld_bb = sem("ld_bb")
        stored = [sem("stored0"), sem("stored1")]
        ident_zero, ident_done, consts_done = sem("ident_zero"), sem("ident_done"), sem("consts_done")
        c_hi_done, c_lo_done = sem("c_hi_done"), sem("c_lo_done")
        stats_done = sem("stats_done")
        rstd_done, rms_done = sem("rstd_done"), sem("rms_done")
        hidden_done, xn_done = sem("hidden_done"), sem("xn_done")
        xt_psum, x_hi_done, x_lo_done = sem("xt_psum"), sem("x_hi_done"), sem("x_lo_done")
        tanh_done, mask_done, valid_done = sem("tanh_done"), sem("mask_done"), sem("valid_done")
        bn_done, ms_done = sem("bn_done"), sem("ms_done")
        qk_hi_done, qk_lo_done = sem("qk_hi_done"), sem("qk_lo_done")
        wv_hi_done, wv_lo_done = sem("wv_hi_done"), sem("wv_lo_done")
        wo_hi_done, wo_lo_done = sem("wo_hi_done"), sem("wo_lo_done")
        q_done, k_done, scores_done, pt_done, pv_done = (sem(n) for n in (
            "q_done", "k_done", "scores_done", "pt_done", "pv_done"))
        q_hi_done, k_hi_done, p_hi_done, a_hi_done = (sem(n) for n in (
            "q_hi_done", "k_hi_done", "p_hi_done", "a_hi_done"))
        q_lo_done, k_lo_done, p_lo_done, a_lo_done = (sem(n) for n in (
            "q_lo_done", "k_lo_done", "p_lo_done", "a_lo_done"))
        small_s_done, small_a_done, exp_done = sem("small_s_done"), sem("small_a_done"), sem("exp_done")
        bm_done, bms_done, a_rest_done = sem("bm_done"), sem("bms_done"), sem("a_rest_done")
        s_done, max_done, rinv_done, rscale_done, norm_done = (sem(n) for n in (
            "s_done", "max_done", "rinv_done", "rscale_done", "norm_done"))
        v_done, v_hi_done, v_lo_done = sem("v_done"), sem("v_hi_done"), sem("v_lo_done")
        o_done, acc_done = sem("o_done"), sem("acc_done")
        f_w_hi, f_w_lo = sem("f_w_hi"), sem("f_w_lo")
        f_x1, f_stat, f_rstd, f_y = sem("f_x1"), sem("f_stat"), sem("f_rstd"), sem("f_y")
        f_yt, f_yhi, f_ylo = sem("f_yt"), sem("f_yhi"), sem("f_ylo")
        f_rl, f_lg, f_chain, f_exp = sem("f_rl"), sem("f_lg"), sem("f_chain"), sem("f_exp")
        f_hw, f_hwt, f_hwhi, f_hwlo = sem("f_hw"), sem("f_hwt"), sem("f_hwhi"), sem("f_hwlo")
        f_base, f_x1b, f_out, f_tb, f_oh = sem("f_base"), sem("f_x1b"), sem("f_out"), sem("f_tb"), sem("f_oh")

        block = ctx.enter_context(nc.Block())

        def reached(eng, s, n):
            if not isinstance(n, int) or n > 0:
                eng.wait_ge(s, n)

        def f32(ap):
            return ap.bitcast(F32)

        def rows(half):
            return slice(half * TH, (half + 1) * TH)

        def tok(j):
            return slice(j * S, (j + 1) * S)

        def out_tiles_before(u, half, p):
            return 2 * (u - p) - 4

        w_base_hi = qk_hi.ap().rearrange("p a b c d -> p (a b c d)").rearrange("p (c n) -> p c n", c=DC)
        w_base_lo = qk_lo.ap().rearrange("p a b c d -> p (a b c d)").rearrange("p (c n) -> p c n", c=DC)
        x_again = [qk_raw.ap().rearrange("p a b c d -> p (a b c d)").rearrange("p (c n) -> p c n", c=DC),
                   stage[:, :, :]]
        y_ring = [small_a[:, :], a_rest[:, :]]
        xn_ring = y_ring
        yT_bank = [QP[:, :], Kb[:, :]]
        RL = [Vb.ap().rearrange("p a b -> p (a b)")[:, 0:2 * RW].rearrange("p (i n) -> p i n", i=2),
              Ob[:, 0:2 * RW].rearrange("p (i n) -> p i n", i=2)]
        base_bank = [Sb.ap().rearrange("p a b c -> p (a b c)")[:, 0:D], Sb.ap().rearrange("p a b c -> p (a b c)")[:, D:2 * D],
                     Ab.ap().rearrange("p a b c -> p (a b c)")[:, 0:D], Ab.ap().rearrange("p a b c -> p (a b c)")[:, D:2 * D]]
        xT_bank = base_bank[2:]
        hw = p_norm
        hwT_hi, hwT_lo = Q_hi, Q_lo
        x1b = [s_sb.ap().rearrange("p a b -> p (a b)"), bm.ap().rearrange("p a b -> p (a b)")]
        out_ring = [p_exp.ap().rearrange("p a b -> p (a b)"), bms.ap().rearrange("p a b -> p (a b)")]

        @block.sync
        def _(sp):
            sp.dma_start(stage[:, :, :], ctxT[:, :, rows(0)]).then_inc(ld_c, 16)
            sp.dma_start(v_raw[:, :, :], wv[0, :, :, :]).then_inc(ld_wv, 16)
            sp.dma_start(acc[:, 0:BH, :], x[:, 0:BH, :]).then_inc(ld_x[0], 16)
            sp.dma_start(qk_raw[:, 0, :, :, :], wqk[0, :, :, :, :]).then_inc(ld_qk[0], 16)
            sp.dma_start(qk_raw[:, 1, :, :, :], wqk[1, :, :, :, :]).then_inc(ld_qk[1], 16)
            sp.dma_start(acc[:, BH:B, :], x[:, BH:B, :]).then_inc(ld_x[1], 16)
            sp.dma_start(o_raw[:, :, :], wo[0, :, :, :]).then_inc(ld_o, 16)
            sp.wait_ge(c_lo_done, DC)
            sp.dma_start(stage[:, :, :], ctxT[:, :, rows(1)]).then_inc(ld_cB, 16)

            def next_group(g):
                sp.wait_ge(qk_lo_done, 2 * g + 1)
                sp.dma_start(qk_raw[:, 0, :, :, :], wqk[2 * g + 2, :, :, :, :]).then_inc(ld_qk[0], 16)
                sp.wait_ge(wv_lo_done, g + 1)
                sp.dma_start(v_raw[:, :, :], wv[g + 1, :, :, :]).then_inc(ld_wv, 16)
                sp.wait_ge(qk_lo_done, 2 * g + 2)
                sp.dma_start(qk_raw[:, 1, :, :, :], wqk[2 * g + 3, :, :, :, :]).then_inc(ld_qk[1], 16)
                sp.wait_ge(bm_done, 4 * g + 3)
                sp.dma_start(bias_sb[:, 0, :], bias[2 * g + 2, :, :]).then_inc(ld_bias[0], 16)
                sp.wait_ge(bm_done, 4 * g + 4)
                sp.dma_start(bias_sb[:, 1, :], bias[2 * g + 3, :, :]).then_inc(ld_bias[1], 16)
                sp.wait_ge(wo_lo_done, g + 1)
                sp.dma_start(o_raw[:, :, :], wo[g + 1, :, :, :]).then_inc(ld_o, 16)

            next_group(0)
            sp.wait_ge(c_lo_done, 2 * DC)
            sp.dma_start(stage[:, :, :], baseT).then_inc(ld_base, 16)
            with sp.Fori(1, G - 1) as g:
                next_group(g)

            sp.wait_ge(xn_done, B)
            sp.dma_start(row_bc[:, :], base_b.broadcast_to([P, D])).then_inc(ld_bb, 16)
            sp.wait_ge(wv_lo_done, G)
            sp.dma_start(v_raw[:, :, 0:RW - 1], loraR).then_inc(ld_lora, 16)
            sp.wait_ge(qk_lo_done, 2 * G)
            sp.dma_start(x_again[0], x[:, 0:BH, :]).then_inc(ld_x2[0], 16)
            sp.wait_ge(wo_lo_done, G)
            sp.dma_start(o_raw[:, 0, :], lora_B).then_inc(ld_loraB, 16)
            sp.wait_ge(f_w_lo, 1)
            sp.dma_start(x_again[1], x[:, BH:B, :]).then_inc(ld_x2[1], 16)
            for j in range(B):
                sp.wait_ge(f_out, j + 1)
                sp.dma_start(out[:, j, :], out_ring[j % 2]).then_inc(stored[j % 2], 16)
            for done in stored:
                sp.wait_ge(done, 16 * (B // 2))

        @block.gpsimd
        def _(pool):
            pool.memset(ident[:, :], 0.0).then_inc(ident_zero, 1)
            pool.memset(half_neg[:, :], -0.5).then_inc(consts_done, 1)
            pool.iota(eidx[:, :], pattern=[[1, E]], base=0, channel_multiplier=0).then_inc(consts_done, 1)
            pool.wait_ge(ident_zero, 1)
            pool.affine_select(out=ident[:, :], in_=ident[:, :], compare_op=ALU.not_equal, fill=1.0,
                               base=0, pattern=[[-1, P]], channel_multiplier=1).then_inc(ident_done, 1)
            pool.wait_ge(consts_done, 2)

            def split_qk_lo(n, p):
                pool.wait_ge(qk_hi_done, n + 1)
                pool.tensor_tensor(qk_lo[:, p, :, :, :], qk_raw[:, p, :, :, :], f32(qk_hi[:, p, :, :, :]),
                                   ALU.subtract).then_inc(qk_lo_done, 1)

            def split_wv_lo(g):
                pool.wait_ge(wv_hi_done, g + 1)
                pool.tensor_tensor(v_lo[:, :, :], v_raw[:, :, :], f32(v_hi[:, :, :]),
                                   ALU.subtract).then_inc(wv_lo_done, 1)

            def split_wo_lo(g):
                pool.wait_ge(wo_hi_done, g + 1)
                pool.tensor_tensor(o_lo[:, :, :], o_raw[:, :, :], f32(o_hi[:, :, :]),
                                   ALU.subtract).then_inc(wo_lo_done, 1)

            def root(h):
                pool.wait_ge(stats_done, 3 * h + 1)
                pool.tensor_tensor(rstd[:, h, :], rstd_in[:, h, :], half_neg[:, :], ALU.pow).then_inc(rstd_done, 1)
                pool.wait_ge(stats_done, 3 * h + 3)
                pool.tensor_tensor(rms_r[:, h, :], rms_in[:, h, :], half_neg[:, :], ALU.pow).then_inc(rms_done, 1)

            def bias_and_mask(g, s):
                t, p, half = 4 * g + s, s % 2, s // 2
                reached(pool, bms_done, t)
                if s < 2:
                    pool.wait_ge(ld_bias[p], 16 * (g + 1))
                if isinstance(g, int) and t == 0:
                    pool.wait_ge(mask_done, 1)
                one = bias_sb[:, p, :].rearrange("p (a k) -> p a k", a=1)
                pool.tensor_tensor(bm[:, :, :], maskneg[:, half * BH:(half + 1) * BH, :],
                                   one.broadcast_to([P, BH, S]), ALU.add).then_inc(bm_done, 1)

            def step(g, s):
                t, first = 4 * g + s, isinstance(g, int) and g == 0
                if not (first and t < 1):
                    reached(pool, s_done, t - 1)
                    pool.wait_ge(small_s_done, t)
                    pool.wait_ge(bm_done, t)
                    pool.tensor_tensor(bms[:, :, :], bm[:, :, :], small_s[:, :, :], ALU.add).then_inc(bms_done, 1)
                if not (first and t < 2):
                    a_remainder(t - 2, ((s - 2) % 4) // 2, s % 2)
                if s == 3:
                    split_wo_lo(g)
                    if not (isinstance(g, int) and g == G - 1):
                        split_qk_lo(2 * g + 2, 0)
                if s == 0:
                    split_qk_lo(2 * g + 1, 1)
                bias_and_mask(g, s)
                if s == 2 and not (isinstance(g, int) and g == G - 1):
                    split_wv_lo(g + 1)

            def a_remainder(u, half, p):
                reached(pool, a_lo_done, u)
                pool.wait_ge(small_a_done, u + 1)
                pool.wait_ge(a_hi_done, u + 1)
                pool.tensor_tensor(a_rest[:, :], small_a[:, :], f32(A_hi[:, half, p, :]),
                                   ALU.subtract).then_inc(a_rest_done, 1)

            root(0)
            split_wv_lo(0)
            split_qk_lo(0, 0)
            step(0, 0)
            root(1)
            for s in range(1, 4):
                step(0, s)
            with pool.Fori(1, G - 1) as g:
                for s in range(4):
                    step(g, s)
            for s in range(4):
                step(G - 1, s)

            reached(pool, s_done, UNITS - 1)
            pool.wait_ge(small_s_done, UNITS)
            pool.wait_ge(bm_done, UNITS)
            pool.tensor_tensor(bms[:, :, :], bm[:, :, :], small_s[:, :, :], ALU.add).then_inc(bms_done, 1)
            for u in (UNITS - 2, UNITS - 1):
                a_remainder(u, 1, u % 2)
            pool.wait_ge(f_w_hi, 1)
            pool.tensor_tensor(w_base_lo, stage[:, :, :], f32(w_base_hi), ALU.subtract).then_inc(f_w_lo, 1)
            pool.wait_ge(f_w_hi, 2)
            pool.tensor_tensor(v_lo[:, :, 0:RW], v_raw[:, :, 0:RW], f32(v_hi[:, :, 0:RW]),
                               ALU.subtract).then_inc(f_w_lo, 1)
            pool.wait_ge(f_w_hi, 3)
            pool.tensor_tensor(o_lo[:, 0, :], o_raw[:, 0, :], f32(o_hi[:, 0, :]), ALU.subtract).then_inc(f_w_lo, 1)
            for h in range(HALVES):
                pool.wait_ge(f_stat, h + 1)
                pool.tensor_tensor(rstd[:, h, :], rstd_in[:, h, :], half_neg[:, :], ALU.pow).then_inc(f_rstd, 1)
            pool.wait_ge(f_tb, 1)
            for j in range(B):
                pool.wait_ge(f_x1, j + 1)
                reached(pool, f_out, j - 1)
                if j < 2:
                    pool.wait_ge(exp_done, UNITS)
                    pool.wait_ge(bms_done, UNITS)
                pool.tensor_tensor(x1b[j % 2], acc[:, j, :], row_bc[:, :], ALU.add).then_inc(f_x1b, 1)

        @block.scalar
        def _(act):
            act.dma_start(row_bc[:, :], lnw.broadcast_to([P, D])).then_inc(ld_lnw, 16)
            act.dma_start(mask8, mask).then_inc(ld_mask, 16)
            act.dma_start(bias_sb[:, 0, :], bias[0, :, :]).then_inc(ld_bias[0], 16)
            act.dma_start(bias_sb[:, 1, :], bias[1, :, :]).then_inc(ld_bias[1], 16)
            act.dma_start(gate[:, 0:1], g_xattn.broadcast_to([P, 1])).then_inc(ld_gate, 16)
            act.dma_start(gate[:, 1:2], g_ffn.broadcast_to([P, 1])).then_inc(ld_gate, 16)
            act.dma_start(rb_bc[:, :], router_b.broadcast_to([P, NR])).then_inc(ld_small, 16)
            act.dma_start(emap[:, :], expert_map.broadcast_to([P, NR])).then_inc(ld_small, 16)

            def high(dst, src, done):
                act.activation(dst, src, ACT.Copy).then_inc(done, 1)

            def context_hi(h):
                act.wait_ge((ld_c, ld_cB)[h], 16)
                for c in range(DC):
                    high(cT_hi[:, c, rows(h)], stage[:, c, :], c_hi_done)

            def x_hi(j):
                act.wait_ge(xt_psum, j + 1)
                high(xT_hi[:, :, tok(j)], xT_bank[j % 2].rearrange("p (c n) -> p c n", c=DC), x_hi_done)

            def split_qk_hi(g, p):
                act.wait_ge(ld_qk[p], 16 * (g + 1))
                reached(act, k_done, 4 * g - 1 + p)
                high(qk_hi[:, p, :, :, :], qk_raw[:, p, :, :, :], qk_hi_done)

            def split_wv_hi(g):
                act.wait_ge(ld_wv, 16 * (g + 1))
                reached(act, v_done, 4 * g)
                high(v_hi[:, :, :], v_raw[:, :, :], wv_hi_done)

            def split_wo_hi(g):
                act.wait_ge(ld_o, 16 * (g + 1))
                reached(act, o_done, 8 * g)
                high(o_hi[:, :, :], o_raw[:, :, :], wo_hi_done)

            def small_scores(u):
                act.wait_ge(scores_done, u + 1)
                reached(act, bms_done, u)
                act.activation(small_s[:, :, :], Sb[:, :, 1, :], ACT.Copy).then_inc(small_s_done, 1)

            def attention_hi(u, half, p):
                act.wait_ge(pv_done, u + 1)
                reached(act, o_done, out_tiles_before(u, half, p))
                high(A_hi[:, half, p, :].rearrange("p (b q) -> p b q", b=BH), Ab[:, :, 0, :], a_hi_done)
                reached(act, a_rest_done, u)
                act.activation(small_a[:, :].rearrange("p (b q) -> p b q", b=BH), Ab[:, :, 1, :],
                               ACT.Copy).then_inc(small_a_done, 1)

            def exponentials(u):
                act.wait_ge(max_done, u + 1)
                reached(act, norm_done, u)
                for i in range(BH):
                    last = act.activation(p_exp[:, i, :], s_sb[:, i, :], ACT.Exp, bias=negmax[:, i:i + 1],
                                          accum_out=rowsum[:, i:i + 1])
                last.then_inc(exp_done, 1)

            def probs_hi(u):
                act.wait_ge(pt_done, u + 1)
                reached(act, pv_done, u)
                high(P_hl[:, :, 0, :], QP[:, :].rearrange("p (b q) -> p b q", b=BH), p_hi_done)

            def v_piece_hi(v, i):
                act.wait_ge(v_done, v + 1)
                if i == 0:
                    reached(act, pv_done, v - 2)
                if i == 2:
                    reached(act, pv_done, v - 2)
                high(V_hi[:, 2 * i:2 * i + 2, :], Vb[:, :, :], v_hi_done)

            def step(g, s):
                t = 4 * g + s
                first, last = (isinstance(g, int) and g == n for n in (0, G - 1))
                if not (first and t < 1):
                    small_scores(t - 1)
                if not (first and t < 2):
                    attention_hi(t - 2, ((s - 2) % 4) // 2, s % 2)
                if s == 3:
                    split_wo_hi(g)
                if not (first and t < 1):
                    exponentials(t - 1)
                act.wait_ge(q_done, t + 1)
                reached(act, scores_done, t)
                high(Q_hi[:, :], QP[:, :], q_hi_done)
                act.wait_ge(k_done, t + 1)
                high(K_hl[:, :, 0, :], Kb[:, :].rearrange("p (b k) -> p b k", b=BH), k_hi_done)
                if s == 3 and not last:
                    split_qk_hi(g + 1, 0)
                if s == 0:
                    split_qk_hi(g, 1)
                if not (first and t < 1):
                    probs_hi(t - 1)
                if not (last and s == 3):
                    v_piece_hi(t + 1, (s + 1) % 4)
                if s == 2 and not last:
                    split_wv_hi(g + 1)

            context_hi(0)
            split_wv_hi(0)
            split_qk_hi(0, 0)
            for j in range(BH):
                x_hi(j)
            v_piece_hi(0, 0)
            step(0, 0)
            context_hi(1)
            for j in range(BH, B):
                x_hi(j)
            step(0, 1)
            act.wait_ge(ld_gate, 32)
            act.activation(tgate[:, :], gate[:, :], ACT.Tanh).then_inc(tanh_done, 1)
            step(0, 2)
            step(0, 3)
            with act.Fori(1, G - 1) as g:
                for s in range(4):
                    step(g, s)
            for s in range(4):
                step(G - 1, s)

            small_scores(UNITS - 1)
            attention_hi(UNITS - 2, 1, 0)
            exponentials(UNITS - 1)
            act.wait_ge(ld_base, 16)
            act.wait_ge(k_done, UNITS)
            high(w_base_hi, stage[:, :, :], f_w_hi)
            probs_hi(UNITS - 1)
            act.wait_ge(ld_lora, 16)
            act.wait_ge(f_oh, 1)
            high(v_hi[:, :, 0:RW], v_raw[:, :, 0:RW], f_w_hi)
            attention_hi(UNITS - 1, 1, 1)
            act.wait_ge(ld_loraB, 16)
            act.wait_ge(o_done, 2 * UNITS)
            high(o_hi[:, 0, :], o_raw[:, 0, :], f_w_hi)

            def y_hi(j):
                act.wait_ge(f_yt, j + 1)
                high(xT_hi[:, :, tok(j)], yT_bank[j % 2].rearrange("p (c n) -> p c n", c=DC), f_yhi)

            def route_exp(h):
                act.wait_ge(f_lg, h + 1)
                act.activation(le[:, :, :], lg[:, :, :], ACT.Exp).then_inc(f_exp, 1)

            def hw_hi(h):
                act.wait_ge(f_hwt, h + 1)
                reached(act, f_base, BH * h)
                high(hwT_hi[:, :], QP[:, :], f_hwhi)

            for j in range(BH):
                y_hi(j)
            route_exp(0)
            for j in range(BH, B):
                y_hi(j)
            hw_hi(0)
            route_exp(1)
            hw_hi(1)

        @block.vector
        def _(dve):
            def low(dst, src, hi, done):
                dve.tensor_tensor(dst, src, f32(hi), ALU.subtract).then_inc(done, 1)

            def context_lo(h):
                for c in range(DC):
                    dve.wait_ge(c_hi_done, DC * h + c + 1)
                    low(cT_lo[:, c, rows(h)], stage[:, c, :], cT_hi[:, c, rows(h)], c_lo_done)

            def layernorm_stats(h):
                dve.wait_ge(ld_x[h], 16)
                for i in range(BH):
                    dve.bn_stats(bn6[:, h, i, :], acc[:, BH * h + i, :]).then_inc(bn_done, 1)
                for i in range(BH):
                    dve.wait_ge(bn_done, 2 * BH * h + i + 1)
                    last = dve.bn_aggr(mv[:, h, i, :], bn6[:, h, i, :]).then_inc(bn_done, 1)
                dve.wait_ge(bn_done, 2 * BH * (h + 1))
                dve.tensor_scalar(rstd_in[:, h, :], mv[:, h, :, 1], LN_EPS, None, ALU.add).then_inc(stats_done, 1)
                dve.wait_ge(rstd_done, h + 1)
                dve.tensor_tensor(rms_in[:, h, :], mv[:, h, :, 1], rstd[:, h, :], ALU.mult).then_inc(ms_done, 1)
                dve.wait_ge(ms_done, h + 1)
                dve.tensor_tensor(rms_in[:, h, :], rms_in[:, h, :], rstd[:, h, :], ALU.mult).then_inc(stats_done, 1)
                dve.wait_ge(stats_done, 3 * h + 2)
                dve.tensor_scalar(rms_in[:, h, :], rms_in[:, h, :], RMS_EPS, None, ALU.add).then_inc(stats_done, 1)
                dve.wait_ge(rms_done, h + 1)

            def normed(j):
                h, i = j // BH, j % BH
                dve.tensor_scalar(acc[:, j, :], acc[:, j, :], mv[:, h, i, 0:1], rstd[:, h, i:i + 1],
                                  ALU.subtract, ALU.mult).then_inc(hidden_done, 1)
                dve.wait_ge(hidden_done, j + 1)
                if j == 0:
                    dve.wait_ge(ld_lnw, 16)
                reached(dve, xt_psum, j - 1)
                dve.scalar_tensor_tensor(out=xn_ring[j % 2], in0=acc[:, j, :], scalar=rms_r[:, h, i:i + 1],
                                         in1=row_bc[:, :], op0=ALU.mult, op1=ALU.mult).then_inc(xn_done, 1)

            def x_lo(j):
                dve.wait_ge(x_hi_done, j + 1)
                low(xT_lo[:, :, tok(j)], xT_bank[j % 2].rearrange("p (c n) -> p c n", c=DC),
                    xT_hi[:, :, tok(j)], x_lo_done)

            def mask_terms():
                dve.wait_ge(ld_mask, 16)
                dve.tensor_reduce(valid[:, :], mask8, AX.X, ALU.max).then_inc(valid_done, 1)
                dve.tensor_scalar(maskneg[:, :, :], mask8, 1.0, MASKED, ALU.subtract, ALU.mult).then_inc(mask_done, 1)

            def scores(u):
                reached(dve, exp_done, u)
                dve.wait_ge(bms_done, u + 1)
                dve.tensor_tensor(s_sb[:, :, :], Sb[:, :, 0, :], bms[:, :, :], ALU.add).then_inc(s_done, 1)
                dve.wait_ge(s_done, u + 1)
                dve.tensor_reduce(negmax[:, :], s_sb[:, :, :], AX.X, ALU.max, negate=True).then_inc(max_done, 1)

            def attention_lo(u, half, p):
                dve.wait_ge(a_rest_done, u + 1)
                dve.tensor_tensor(A_lo[:, half, p, :].rearrange("p (b q) -> p b q", b=BH), Ab[:, :, 0, :],
                                  a_rest[:, :].rearrange("p (b q) -> p b q", b=BH), ALU.add).then_inc(a_lo_done, 1)

            def normalise(u, half):
                dve.wait_ge(exp_done, u + 1)
                dve.reciprocal(rinv[:, :], rowsum[:, :]).then_inc(rinv_done, 1)
                dve.wait_ge(rinv_done, u + 1)
                dve.tensor_tensor(rscale[:, :], rinv[:, :], valid[:, half * BH:(half + 1) * BH],
                                  ALU.mult).then_inc(rscale_done, 1)
                dve.wait_ge(rscale_done, u + 1)
                reached(dve, pt_done, u)
                scale = rscale[:, :].rearrange("p (b o) -> p b o", o=1).broadcast_to([P, BH, S])
                dve.tensor_tensor(p_norm[:, :, :], p_exp[:, :, :], scale, ALU.mult).then_inc(norm_done, 1)

            def probs_lo(u):
                dve.wait_ge(p_hi_done, u + 1)
                low(P_hl[:, :, 1, :], QP[:, :].rearrange("p (b q) -> p b q", b=BH), P_hl[:, :, 0, :], p_lo_done)

            def v_piece_lo(v, i):
                dve.wait_ge(v_hi_done, v + 1)
                low(V_lo[:, 2 * i:2 * i + 2, :], Vb[:, :, :], V_hi[:, 2 * i:2 * i + 2, :], v_lo_done)

            def add_out(n, j):
                dve.wait_ge(o_done, n + 1)
                dve.tensor_tensor(acc[:, j, :], Ob[:, :], acc[:, j, :], ALU.add).then_inc(acc_done, 1)

            def step(g, s):
                t = 4 * g + s
                first, last = (isinstance(g, int) and g == n for n in (0, G - 1))
                if not (first and t < 1):
                    scores(t - 1)
                if not (first and t < 2):
                    attention_lo(t - 2, ((s - 2) % 4) // 2, s % 2)
                if not (first and t < 1):
                    normalise(t - 1, ((s - 1) % 4) // 2)
                dve.wait_ge(q_hi_done, t + 1)
                low(Q_lo[:, :], QP[:, :], Q_hi[:, :], q_lo_done)
                dve.wait_ge(k_hi_done, t + 1)
                low(K_hl[:, :, 1, :], Kb[:, :].rearrange("p (b k) -> p b k", b=BH), K_hl[:, :, 0, :], k_lo_done)
                o, j = t - 3, 2 * ((s - 3) % 4)
                if not (first and t < 3):
                    add_out(2 * o, j)
                if not (first and t < 1):
                    probs_lo(t - 1)
                if not (last and s == 3):
                    v_piece_lo(t + 1, (s + 1) % 4)
                if not (first and t < 3):
                    add_out(2 * o + 1, j + 1)

            context_lo(0)
            layernorm_stats(0)
            for j in range(BH):
                normed(j)
                if j >= 1:
                    x_lo(j - 1)
            mask_terms()
            x_lo(BH - 1)
            v_piece_lo(0, 0)
            step(0, 0)
            context_lo(1)
            layernorm_stats(1)
            for j in range(BH, B):
                normed(j)
                if j > BH:
                    x_lo(j - 1)
            x_lo(B - 1)
            step(0, 1)
            step(0, 2)
            step(0, 3)
            with dve.Fori(1, G - 1) as g:
                for s in range(4):
                    step(g, s)
            for s in range(4):
                step(G - 1, s)

            chained = [0]

            def tick(ins):
                chained[0] += 1
                ins.then_inc(f_chain, 1)
                dve.wait_ge(f_chain, chained[0])

            def x1(j):
                h, i = j // BH, j % BH
                dve.wait_ge(acc_done, 2 * UNITS - B + j + 1)
                if i == 0:
                    dve.wait_ge(ld_x2[h], 16)
                    dve.wait_ge(tanh_done, 1)
                dve.scalar_tensor_tensor(out=acc[:, j, :], in0=acc[:, j, :], scalar=tgate[:, 0:1],
                                         in1=x_again[h][:, i, :], op0=ALU.mult, op1=ALU.add).then_inc(f_x1, 1)
                dve.wait_ge(f_x1, j + 1)
                tick(dve.bn_stats(bn6[:, h, i, :], acc[:, j, :]))
                tick(dve.bn_aggr(mv[:, h, i, :], bn6[:, h, i, :]))

            def ffn_rstd_in(h):
                dve.tensor_scalar(rstd_in[:, h, :], mv[:, h, :, 1], LN_EPS, None, ALU.add).then_inc(f_stat, 1)

            def y(j):
                h, i = j // BH, j % BH
                if i == 0:
                    dve.wait_ge(f_rstd, h + 1)
                if j < 2:
                    dve.wait_ge(a_lo_done, UNITS)
                reached(dve, f_yt, j - 1)
                dve.tensor_scalar(y_ring[j % 2], acc[:, j, :], mv[:, h, i, 0:1], rstd[:, h, i:i + 1],
                                  ALU.subtract, ALU.mult).then_inc(f_y, 1)

            def y_lo(j):
                dve.wait_ge(f_yhi, j + 1)
                low(xT_lo[:, :, tok(j)], yT_bank[j % 2].rearrange("p (c n) -> p c n", c=DC),
                    xT_hi[:, :, tok(j)], f_ylo)

            def router_constants():
                dve.wait_ge(ld_small, 32)
                dve.wait_ge(consts_done, 2)
                tick(dve.tensor_copy(emap_f[:, :], emap[:, :]))
                tick(dve.tensor_copy(eidx_f[:, :], eidx[:, :]))
                for e in range(E):
                    ins = dve.tensor_scalar(onehot[:, e, :], emap_f[:, :], eidx_f[:, e:e + 1], LORA_SCALE,
                                            ALU.is_equal, ALU.mult)
                tick(ins)
                dve.wait_ge(wv_lo_done, G)
                dve.memset(v_raw[:, :, RW - 1:RW], 0.0).then_inc(f_oh, 1)
                dve.wait_ge(ld_bb, 16)
                dve.wait_ge(tanh_done, 1)
                dve.tensor_scalar(row_bc[:, :], row_bc[:, :], tgate[:, 1:2], None, ALU.mult).then_inc(f_tb, 1)

            def route(h):
                for k in range(2):
                    dve.wait_ge(f_rl, 2 * h + k + 1)
                    bc = rb_bc[:, :].rearrange("p (a n) -> p a n", a=1).broadcast_to([P, 2, NR])
                    tick(dve.tensor_tensor(lg[:, 2 * k:2 * k + 2, :], RL[k][:, :, ER:ER + NR], bc, ALU.add))
                tick(dve.tensor_reduce(lmax[:, :], lg[:, :, :], AX.X, ALU.max))
                top = lmax[:, :].rearrange("p (b o) -> p b o", o=1).broadcast_to([P, BH, NR])
                dve.tensor_tensor(lg[:, :, :], lg[:, :, :], top, ALU.subtract).then_inc(f_lg, 1)
                dve.wait_ge(f_exp, h + 1)
                tick(dve.tensor_reduce(lsum[:, :], le[:, :, :], AX.X, ALU.add))
                tick(dve.reciprocal(lrec[:, :], lsum[:, :]))
                inv = lrec[:, :].rearrange("p (b o) -> p b o", o=1).broadcast_to([P, BH, NR])
                tick(dve.tensor_tensor(probs[:, :, :], le[:, :, :], inv, ALU.mult))
                for i in range(BH):
                    ins = dve.max(top8[:, i, :], probs[:, i, :])
                tick(ins)
                for i in range(BH):
                    ins = dve.match_replace(rest[:, i, :], top8[:, i, :], probs[:, i, :], 0.0)
                tick(ins)
                tick(dve.tensor_tensor(chosen[:, :, :], probs[:, :, :], rest[:, :, :], ALU.subtract))
                for i in range(BH):
                    sel = chosen[:, i, :].rearrange("p (a n) -> p a n", a=1).broadcast_to([P, E, NR])
                    ins = dve.tensor_tensor(picked[:, i, :, :], sel, onehot[:, :, :], ALU.mult)
                tick(ins)
                tick(dve.tensor_reduce(we[:, :, :], picked[:, :, :, :], AX.X, ALU.add))
                reached(dve, f_hwt, h)
                for i in range(BH):
                    w = we[:, i, :].rearrange("p (e o) -> p e o", o=1).broadcast_to([P, E, R])
                    ins = dve.tensor_tensor(hw[:, i, :].rearrange("p (e r) -> p e r", e=E),
                                            RL[i // 2][:, i % 2, 0:ER].rearrange("p (e r) -> p e r", e=E), w, ALU.mult)
                ins.then_inc(f_hw, 1)

            def hw_lo(h):
                dve.wait_ge(f_hwhi, h + 1)
                low(hwT_lo[:, :], QP[:, :], hwT_hi[:, :], f_hwlo)

            def result(j):
                dve.wait_ge(f_base, j + 1)
                dve.wait_ge(f_x1b, j + 1)
                reached(dve, stored[j % 2], 16 * (j // 2))
                dve.scalar_tensor_tensor(out=out_ring[j % 2], in0=base_bank[j % BH], scalar=tgate[:, 1:2],
                                         in1=x1b[j % 2], op0=ALU.mult, op1=ALU.add).then_inc(f_out, 1)

            scores(UNITS - 1)
            attention_lo(UNITS - 2, 1, 0)
            normalise(UNITS - 1, 1)
            add_out(2 * UNITS - 6, 2)
            probs_lo(UNITS - 1)
            add_out(2 * UNITS - 5, 3)
            router_constants()
            x1(0)
            attention_lo(UNITS - 1, 1, 1)
            x1(1)
            add_out(2 * UNITS - 4, 4)
            x1(2)
            add_out(2 * UNITS - 3, 5)
            x1(3)
            ffn_rstd_in(0)
            add_out(2 * UNITS - 2, 6)
            add_out(2 * UNITS - 1, 7)
            y(0)
            y(1)
            y_lo(0)
            y(2)
            y_lo(1)
            y(3)
            y_lo(2)
            y_lo(3)
            for j in range(BH, B):
                x1(j)
            ffn_rstd_in(1)
            route(0)
            y(4)
            y(5)
            y_lo(4)
            y(6)
            y_lo(5)
            y(7)
            y_lo(6)
            y_lo(7)
            hw_lo(0)
            for j in range(BH):
                result(j)
            route(1)
            hw_lo(1)
            for j in range(BH, B):
                result(j)

        @block.tensor
        def _(pe):
            def product(dst, w_hi, w_lo, m_hi, m_lo, start, stop):
                pe.matmul(dst, w_lo, m_hi, start=start, stop=False)
                pe.matmul(dst, w_hi, m_lo, start=False, stop=False)
                return pe.matmul(dst, w_hi, m_hi, start=False, stop=stop)

            def x_transpose(j):
                pe.wait_ge(xn_done, j + 1)
                reached(pe, x_lo_done, j - 1)
                for c in range(DC):
                    last = pe.transpose(xT_bank[j % 2][:, c * P:(c + 1) * P], xn_ring[j % 2][:, c * P:(c + 1) * P],
                                        ident[:, :])
                last.then_inc(xt_psum, 1)

            def project(bank, p, which, source_hi, source_lo, half, done):
                for c in range(DC):
                    last = product(bank, qk_hi[:, p, which, c, :], qk_lo[:, p, which, c, :],
                                   source_hi[:, c, rows(half)], source_lo[:, c, rows(half)], c == 0, c == DC - 1)
                last.then_inc(done, 1)

            def v_piece(v, g, i):
                reached(pe, v_lo_done, v)
                if i == 0:
                    pe.wait_ge(wv_lo_done, g + 1)
                for k in range(2):
                    j = 2 * i + k
                    for c in range(DC):
                        last = product(Vb[:, k, :], cT_hi[:, c, tok(j)], cT_lo[:, c, tok(j)],
                                       v_hi[:, c, :], v_lo[:, c, :], c == 0, c == DC - 1)
                last.then_inc(v_done, 1)

            def out_tile(n, g, j):
                reached(pe, acc_done, n)
                half, b = j // BH, j % BH
                if j == 0:
                    pe.wait_ge(wo_lo_done, g + 1)
                if j % BH == 0:
                    pe.wait_ge(a_lo_done, 4 * g + 2 * half + 2)
                for p in range(2):
                    last = product(Ob[:, :], A_hi[:, half, p, tok(b)], A_lo[:, half, p, tok(b)],
                                   o_hi[:, p, :], o_lo[:, p, :], p == 0, p == 1)
                last.then_inc(o_done, 1)

            def transpose_probs(u):
                pe.wait_ge(norm_done, u + 1)
                for b in range(BH):
                    last = pe.transpose(QP[:, tok(b)], p_norm[:, b, :], ident[:, :])
                last.then_inc(pt_done, 1)

            def scores(u):
                pe.wait_ge(q_lo_done, u + 1)
                pe.wait_ge(k_lo_done, u + 1)
                reached(pe, s_done, u)
                reached(pe, small_s_done, u)
                for b in range(BH):
                    pe.matmul(Sb[:, b, :, :], Q_hi[:, tok(b)], K_hl[:, b, :, :], start=True, stop=False)
                    last = pe.matmul(Sb[:, b, 0, :], Q_lo[:, tok(b)], K_hl[:, b, 0, :], start=False, stop=True)
                last.then_inc(scores_done, 1)

            def apply_probs(u, half, p, v_pieces):
                pe.wait_ge(p_lo_done, u + 1)
                pe.wait_ge(v_lo_done, v_pieces)
                reached(pe, a_lo_done, u)
                reached(pe, small_a_done, u)
                for b in range(BH):
                    j, cols = BH * half + b, slice(p * DH, (p + 1) * DH)
                    pe.matmul(Ab[:, b, :, :], V_hi[:, j, cols], P_hl[:, b, :, :], start=True, stop=False)
                    last = pe.matmul(Ab[:, b, 0, :], V_lo[:, j, cols], P_hl[:, b, 0, :], start=False, stop=True)
                last.then_inc(pv_done, 1)

            def step(g, s):
                t, p, half = 4 * g + s, s % 2, s // 2
                first, last = (isinstance(g, int) and g == n for n in (0, G - 1))
                if s < 2:
                    pe.wait_ge(qk_lo_done, 2 * g + p + 1)
                reached(pe, p_lo_done, t - 1)
                project(QP[:, :], p, 0, xT_hi, xT_lo, half, q_done)
                reached(pe, k_lo_done, t)
                project(Kb[:, :], p, 1, cT_hi, cT_lo, half, k_done)
                o, j = t - 3, 2 * ((s - 3) % 4)
                og = g if s == 3 else g - 1
                if not (first and t < 3):
                    out_tile(2 * o, og, j)
                if not (last and s == 3):
                    v_piece(t + 1, g + (s == 3), (s + 1) % 4)
                if not (first and t < 1):
                    pe.wait_ge(q_lo_done, t + 1)
                    transpose_probs(t - 1)
                if not (first and t < 3):
                    out_tile(2 * o + 1, og, j + 1)
                scores(t)
                if not (first and t < 1):
                    u_half, u_p = ((s - 1) % 4) // 2, (s - 1) % 2
                    u_g4 = 4 * (g if s > 0 else g - 1)
                    apply_probs(t - 1, u_half, u_p, u_g4 + 2 * u_half + 2)

            pe.wait_ge(c_lo_done, DC)
            v_piece(0, 0, 0)
            pe.wait_ge(ident_done, 1)
            for j in range(BH):
                x_transpose(j)
            pe.wait_ge(x_lo_done, BH)
            step(0, 0)
            pe.wait_ge(c_lo_done, 2 * DC)
            for j in range(BH, B):
                x_transpose(j)
            step(0, 1)
            pe.wait_ge(x_lo_done, B)
            step(0, 2)
            step(0, 3)
            with pe.Fori(1, G - 1) as g:
                for s in range(4):
                    step(g, s)
            for s in range(4):
                step(G - 1, s)

            out_tile(2 * UNITS - 6, G - 1, 2)
            transpose_probs(UNITS - 1)
            out_tile(2 * UNITS - 5, G - 1, 3)
            apply_probs(UNITS - 1, 1, 1, UNITS)
            for j in range(4, 8):
                out_tile(2 * UNITS - B + j, G - 1, j)

            def y_transpose(j):
                pe.wait_ge(f_y, j + 1)
                reached(pe, f_ylo, j - 1)
                if j == 0:
                    pe.wait_ge(p_lo_done, UNITS)
                for c in range(DC):
                    last = pe.transpose(yT_bank[j % 2][:, c * P:(c + 1) * P], y_ring[j % 2][:, c * P:(c + 1) * P],
                                        ident[:, :])
                last.then_inc(f_yt, 1)

            def lora_and_router(h):
                pe.wait_ge(f_w_lo, 2)
                reached(pe, f_hw, h)
                if h == 0:
                    pe.wait_ge(acc_done, 2 * UNITS)
                for i in range(BH):
                    j = BH * h + i
                    pe.wait_ge(f_ylo, j + 1)
                    for c in range(DC):
                        last = product(RL[i // 2][:, i % 2, :], xT_hi[:, c, tok(j)], xT_lo[:, c, tok(j)],
                                       v_hi[:, c, 0:RW], v_lo[:, c, 0:RW], c == 0, c == DC - 1)
                    if i % 2:
                        last.then_inc(f_rl, 1)

            def base(h):
                pe.wait_ge(f_w_lo, 1)
                for i in range(BH):
                    j = BH * h + i
                    if h == 0 and i == 2:
                        pe.wait_ge(a_lo_done, UNITS)
                    reached(pe, f_out, j - BH + 1)
                    for c in range(DC):
                        product(base_bank[i], xT_hi[:, c, tok(j)], xT_lo[:, c, tok(j)],
                                w_base_hi[:, c, :], w_base_lo[:, c, :], c == 0, False)

            def hw_transpose(h):
                pe.wait_ge(f_hw, h + 1)
                pe.wait_ge(f_ylo, B)
                for i in range(BH):
                    last = pe.transpose(QP[:, tok(i)], hw[:, i, :], ident[:, :])
                last.then_inc(f_hwt, 1)

            def lora_out(h):
                pe.wait_ge(f_hwlo, h + 1)
                pe.wait_ge(f_w_lo, 3)
                for i in range(BH):
                    product(base_bank[i], hwT_hi[:, tok(i)], hwT_lo[:, tok(i)], o_hi[:, 0, :], o_lo[:, 0, :],
                            False, True).then_inc(f_base, 1)

            for j in range(BH):
                y_transpose(j)
            lora_and_router(0)
            base(0)
            for j in range(BH, B):
                y_transpose(j)
            hw_transpose(0)
            lora_out(0)
            lora_and_router(1)
            base(1)
            hw_transpose(1)
            lora_out(1)


_INPUTS = ["x", "ctxT", "mask", "g_xattn", "g_ffn", "bias", "lnw", "wqk", "wv", "wo", "baseT", "base_b",
           "loraR", "router_b", "lora_B", "expert_map"]


def kernel(x, ctx_4096, mask_BxSxS2_bk0, g_xattn, g_ffn, L0_xattn_position_bias, L0_xattn_ln_weight,
           L0_xattn_w_q, L0_xattn_w_k, L0_xattn_w_v, L0_xattn_w_out, L0_ffn_base_W, L0_ffn_base_b,
           L0_ffn_router_W, L0_ffn_router_b, L0_ffn_A, L0_ffn_B, L0_ffn_expert_map):
    import numpy as np
    import concourse.bacc as bacc
    from concourse.bass_utils import run_bass_kernel_spmd

    def by_chunk(w):
        return np.asarray(w).reshape(-1, DC, P).transpose(2, 1, 0)

    def heads(w, n):
        return np.asarray(w).reshape(H // n, n * DH, DC, P).transpose(0, 3, 2, 1)

    given = {
        "x": np.asarray(x).transpose(1, 0, 2),
        "ctxT": by_chunk(np.asarray(ctx_4096).reshape(B * S, D)),
        "mask": np.asarray(mask_BxSxS2_bk0).transpose(1, 0, 2),
        "g_xattn": np.asarray(g_xattn).reshape(1, 1),
        "g_ffn": np.asarray(g_ffn).reshape(1, 1),
        "bias": np.asarray(L0_xattn_position_bias),
        "lnw": np.asarray(L0_xattn_ln_weight).reshape(1, D),
        "wqk": np.stack([heads(L0_xattn_w_q, 1), heads(L0_xattn_w_k, 1)], axis=2),
        "wv": heads(L0_xattn_w_v, 2),
        "wo": np.asarray(L0_xattn_w_out).reshape(D, G, 2, DH).transpose(1, 3, 2, 0),
        "baseT": by_chunk(L0_ffn_base_W),
        "base_b": np.asarray(L0_ffn_base_b).reshape(1, D),
        "loraR": np.concatenate([by_chunk(np.asarray(L0_ffn_A).reshape(ER, D)), by_chunk(L0_ffn_router_W)], axis=2),
        "router_b": np.asarray(L0_ffn_router_b).reshape(1, NR),
        "lora_B": np.asarray(L0_ffn_B).transpose(0, 2, 1).reshape(ER, D),
        "expert_map": np.asarray(L0_ffn_expert_map).reshape(1, NR),
    }
    given = {name: np.ascontiguousarray(a) for name, a in given.items()}

    nc = bacc.Bacc("TRN2", target_bir_lowering=False, num_devices=1)
    args = [nc.dram_tensor(n, given[n].shape, mybir.dt.from_np(given[n].dtype), kind="ExternalInput").ap()
            for n in _INPUTS]
    args.append(nc.dram_tensor("out", (P, B, D), F32, kind="ExternalOutput").ap())
    build(nc, *args)
    result = run_bass_kernel_spmd(nc, [given], core_ids=[0]).results[0]["out"]
    return result.transpose(1, 0, 2)
```

```python
from contextlib import ExitStack

import concourse.bass as bass
from concourse import mybir

F32 = mybir.dt.float32
F32R = mybir.dt.float32r
U8 = mybir.dt.uint8
I32 = mybir.dt.int32
ALU = mybir.AluOpType
ACT = mybir.ActivationFunctionType
AX = mybir.AxisListType

P = 128
B, S, D = 8, 128, 512
H, DH = 32, 128
DC = D // P
HALVES = 2
BH = B // HALVES
TH = BH * S
G = H // 2
UNITS = 4 * G
NR, E, R = 15, 8, 16
ER = E * R
RW = ER + 16
LN_EPS = 1e-5
RMS_EPS = 1e-5
LORA_SCALE = 2.0
MASKED = 2.0 ** 100


def build(nc, x, ctxT, mask, g_xattn, g_ffn, bias, lnw, wqk, wv, wo, baseT, base_b, loraR, router_b,
          lora_B, expert_map, out):
    with ExitStack() as ctx:
        def sb(name, shape, dt=F32):
            return ctx.enter_context(nc.sbuf_tensor(name, shape, dt))

        def psum(name, shape):
            return ctx.enter_context(nc.psum_tensor(name, shape, F32))

        def sem(name):
            return ctx.enter_context(nc.semaphore(name))

        xT_hi, xT_lo = sb("xT_hi", [P, DC, B * S], F32R), sb("xT_lo", [P, DC, B * S], F32R)
        cT_hi, cT_lo = sb("cT_hi", [P, DC, B * S], F32R), sb("cT_lo", [P, DC, B * S], F32R)
        acc = sb("acc", [P, B, D])
        qk_raw = sb("qk_raw", [P, 2, 2, DC, DH])
        qk_hi, qk_lo = sb("qk_hi", [P, 2, 2, DC, DH], F32R), sb("qk_lo", [P, 2, 2, DC, DH], F32R)
        v_raw = sb("v_raw", [P, DC, 2 * DH])
        v_hi, v_lo = sb("v_hi", [P, DC, 2 * DH], F32R), sb("v_lo", [P, DC, 2 * DH], F32R)
        o_raw = sb("o_raw", [P, 2, D])
        o_hi, o_lo = sb("o_hi", [P, 2, D], F32R), sb("o_lo", [P, 2, D], F32R)
        V_hi, V_lo = sb("V_hi", [P, B, 2 * DH], F32R), sb("V_lo", [P, B, 2 * DH], F32R)
        A_hi, A_lo = sb("A_hi", [P, HALVES, 2, TH], F32R), sb("A_lo", [P, HALVES, 2, TH], F32R)
        Q_hi, Q_lo = sb("Q_hi", [P, TH], F32R), sb("Q_lo", [P, TH], F32R)
        K_hl = sb("K_hl", [P, BH, 2, S], F32R)
        P_hl = sb("P_hl", [P, BH, 2, S], F32R)
        bias_sb = sb("bias_sb", [P, 2, S])
        maskneg = sb("maskneg", [P, B, S])
        bm = sb("bm", [P, BH, S])
        bms = sb("bms", [P, BH, S])
        small_s = sb("small_s", [P, BH, S])
        s_sb = sb("s_sb", [P, BH, S])
        p_exp = sb("p_exp", [P, BH, S])
        p_norm = sb("p_norm", [P, BH, S])
        small_a = sb("small_a", [P, TH])
        a_rest = sb("a_rest", [P, TH])
        stage = sb("stage", [P, DC, D])
        row_bc = sb("row_bc", [P, D])
        ident = sb("ident", [P, P])
        valid = sb("valid", [P, B])
        negmax, rowsum = sb("negmax", [P, BH]), sb("rowsum", [P, BH])
        rinv, rscale = sb("rinv", [P, BH]), sb("rscale", [P, BH])
        gate = sb("gate", [P, 2])
        tgate = sb("tgate", [P, 2])
        half_neg = sb("half_neg", [P, BH])
        bn6 = sb("bn6", [P, 2, BH, 6])
        mv = sb("mv", [P, 2, BH, 2])
        rstd_in, rstd = sb("rstd_in", [P, 2, BH]), sb("rstd", [P, 2, BH])
        rms_in, rms_r = sb("rms_in", [P, 2, BH]), sb("rms_r", [P, 2, BH])
        mask8 = p_norm.ap().rearrange("p a b -> p (a b)")[:, 0:B * S // 4].bitcast(U8)
        mask8 = mask8.rearrange("p (b k) -> p b k", b=B)
        rb_bc = sb("rb_bc", [P, NR])
        emap = sb("emap", [P, NR], I32)
        emap_f = sb("emap_f", [P, NR])
        eidx = sb("eidx", [P, E], I32)
        eidx_f = sb("eidx_f", [P, E])
        onehot = sb("onehot", [P, E, NR])
        lg = sb("lg", [P, BH, NR])
        lmax, lsum, lrec = sb("lmax", [P, BH]), sb("lsum", [P, BH]), sb("lrec", [P, BH])
        le, probs = sb("le", [P, BH, NR]), sb("probs", [P, BH, NR])
        top8 = sb("top8", [P, BH, 8])
        rest = sb("rest", [P, BH, NR])
        chosen = sb("chosen", [P, BH, NR])
        picked = small_s.ap().rearrange("p a b -> p (a b)")[:, 0:BH * E * NR]
        picked = picked.rearrange("p (i e n) -> p i e n", i=BH, e=E)
        we = sb("we", [P, BH, E])

        QP = psum("QP", [P, TH])
        Kb = psum("Kb", [P, TH])
        Vb = psum("Vb", [P, 2, 2 * DH])
        Ob = psum("Ob", [P, D])
        Sb = psum("Sb", [P, BH, 2, S])
        Ab = psum("Ab", [P, BH, 2, S])

        ld_c = [sem(f"ld_c{c}") for c in range(DC)] + [sem("ld_cB")]
        ld_x = [sem(f"ld_x{j}") for j in range(BH)] + [sem("ld_xB")]
        ld_o = sem("ld_o")
        ld_wv = sem("ld_wv")
        ld_qk = [sem("ld_qk0"), sem("ld_qk1")]
        ld_bias = [sem("ld_bias0"), sem("ld_bias1")]
        ld_lnw, ld_mask, ld_gate = sem("ld_lnw"), sem("ld_mask"), sem("ld_gate")
        ld_small, ld_base, ld_lora, ld_loraB = sem("ld_small"), sem("ld_base"), sem("ld_lora"), sem("ld_loraB")
        ld_x2 = [sem("ld_x2A"), sem("ld_x2B")]
        ld_bb = sem("ld_bb")
        stored = [sem("stored0"), sem("stored1")]
        ident_zero, ident_done, consts_done = sem("ident_zero"), sem("ident_done"), sem("consts_done")
        c_hi_done, c_lo_done = sem("c_hi_done"), sem("c_lo_done")
        stats_done = sem("stats_done")
        rstd_done, rms_done = sem("rstd_done"), sem("rms_done")
        hidden_done, xn_done = sem("hidden_done"), sem("xn_done")
        xt_psum, x_hi_done, x_lo_done = sem("xt_psum"), sem("x_hi_done"), sem("x_lo_done")
        tanh_done, mask_done, valid_done = sem("tanh_done"), sem("mask_done"), sem("valid_done")
        bn_done, ms_done = sem("bn_done"), sem("ms_done")
        qk_hi_done, qk_lo_done = sem("qk_hi_done"), sem("qk_lo_done")
        wv_hi_done, wv_lo_done = sem("wv_hi_done"), sem("wv_lo_done")
        wo_hi_done, wo_lo_done = sem("wo_hi_done"), sem("wo_lo_done")
        q_done, k_done, scores_done, pt_done, pv_done = (sem(n) for n in (
            "q_done", "k_done", "scores_done", "pt_done", "pv_done"))
        q_hi_done, k_hi_done, p_hi_done, a_hi_done = (sem(n) for n in (
            "q_hi_done", "k_hi_done", "p_hi_done", "a_hi_done"))
        q_lo_done, k_lo_done, p_lo_done, a_lo_done = (sem(n) for n in (
            "q_lo_done", "k_lo_done", "p_lo_done", "a_lo_done"))
        small_s_done, small_a_done, exp_done = sem("small_s_done"), sem("small_a_done"), sem("exp_done")
        bm_done, bms_done, a_rest_done = sem("bm_done"), sem("bms_done"), sem("a_rest_done")
        s_done, max_done, rinv_done, rscale_done, norm_done = (sem(n) for n in (
            "s_done", "max_done", "rinv_done", "rscale_done", "norm_done"))
        v_done, v_hi_done, v_lo_done = sem("v_done"), sem("v_hi_done"), sem("v_lo_done")
        o_done, acc_done = sem("o_done"), sem("acc_done")
        f_w_hi, f_w_lo = sem("f_w_hi"), sem("f_w_lo")
        f_x1, f_stat, f_rstd, f_y = sem("f_x1"), sem("f_stat"), sem("f_rstd"), sem("f_y")
        f_yt, f_yhi, f_ylo = sem("f_yt"), sem("f_yhi"), sem("f_ylo")
        f_rl, f_lg, f_chain, f_exp = sem("f_rl"), sem("f_lg"), sem("f_chain"), sem("f_exp")
        f_hw, f_hwt, f_hwhi, f_hwlo = sem("f_hw"), sem("f_hwt"), sem("f_hwhi"), sem("f_hwlo")
        f_base, f_x1b, f_out, f_tb = sem("f_base"), sem("f_x1b"), sem("f_out"), sem("f_tb")

        block = ctx.enter_context(nc.Block())

        def reached(eng, s, n):
            if not isinstance(n, int) or n > 0:
                eng.wait_ge(s, n)

        def f32(ap):
            return ap.bitcast(F32)

        def rows(half):
            return slice(half * TH, (half + 1) * TH)

        def tok(j):
            return slice(j * S, (j + 1) * S)

        def out_tiles_before(u, half, p):
            return 2 * (u - p) - 4

        w_base_hi = qk_hi.ap().rearrange("p a b c d -> p (a b c d)").rearrange("p (c n) -> p c n", c=DC)
        w_base_lo = qk_lo.ap().rearrange("p a b c d -> p (a b c d)").rearrange("p (c n) -> p c n", c=DC)
        x_again = [qk_raw.ap().rearrange("p a b c d -> p (a b c d)").rearrange("p (c n) -> p c n", c=DC),
                   stage[:, :, :]]
        y_ring = [v_raw.ap().rearrange("p a b -> p (a b)")[:, 0:D], v_raw.ap().rearrange("p a b -> p (a b)")[:, D:2 * D]]
        xn_ring = [small_a[:, :], a_rest[:, :]]
        w_loraB_hi = V_hi[:, 0:2, :].rearrange("p a b -> p (a b)")
        w_loraB_lo = V_lo[:, 0:2, :].rearrange("p a b -> p (a b)")
        yT_bank = [QP[:, :], Kb[:, :]]
        RL = [Vb.ap().rearrange("p a b -> p (a b)")[:, 0:2 * RW].rearrange("p (i n) -> p i n", i=2),
              Ob[:, 0:2 * RW].rearrange("p (i n) -> p i n", i=2)]
        base_bank = [Sb.ap().rearrange("p a b c -> p (a b c)")[:, 0:D], Sb.ap().rearrange("p a b c -> p (a b c)")[:, D:2 * D],
                     Ab.ap().rearrange("p a b c -> p (a b c)")[:, 0:D], Ab.ap().rearrange("p a b c -> p (a b c)")[:, D:2 * D]]
        xT_bank = 3 * base_bank[2:] + 2 * [Ob[:, :]]
        late_bank = {2 * UNITS - 7: Vb.ap().rearrange("p a b -> p (a b)"), 2 * UNITS - 5: Vb.ap().rearrange("p a b -> p (a b)"),
                     2 * UNITS - 4: QP[:, :], 2 * UNITS - 3: Kb[:, :], 2 * UNITS - 2: QP[:, :], 2 * UNITS - 1: Kb[:, :]}
        hw = p_norm
        hwT_hi, hwT_lo = Q_hi, Q_lo
        x1b = [s_sb.ap().rearrange("p a b -> p (a b)"), bm.ap().rearrange("p a b -> p (a b)")]
        out_ring = [p_exp.ap().rearrange("p a b -> p (a b)"), bms.ap().rearrange("p a b -> p (a b)")]

        @block.sync
        def _(sp):
            for j in range(BH):
                sp.dma_start(acc[:, j, :], x[:, j, :]).then_inc(ld_x[j], 16)
            for c in range(DC):
                sp.dma_start(stage[:, c, :], ctxT[:, c, rows(0)]).then_inc(ld_c[c], 16)
            sp.dma_start(v_raw[:, :, :], wv[0, :, :, :]).then_inc(ld_wv, 16)
            sp.dma_start(row_bc[:, :], lnw.broadcast_to([P, D])).then_inc(ld_lnw, 16)
            sp.dma_start(qk_raw[:, 0, :, :, :], wqk[0, :, :, :, :]).then_inc(ld_qk[0], 16)
            sp.dma_start(mask8, mask).then_inc(ld_mask, 16)
            sp.dma_start(acc[:, BH:B, :], x[:, BH:B, :]).then_inc(ld_x[BH], 16)
            sp.dma_start(qk_raw[:, 1, :, :, :], wqk[1, :, :, :, :]).then_inc(ld_qk[1], 16)
            sp.dma_start(bias_sb[:, 0, :], bias[0, :, :]).then_inc(ld_bias[0], 16)
            sp.wait_ge(c_lo_done, DC)
            sp.dma_start(stage[:, :, :], ctxT[:, :, rows(1)]).then_inc(ld_c[DC], 16)
            sp.dma_start(bias_sb[:, 1, :], bias[1, :, :]).then_inc(ld_bias[1], 16)
            sp.dma_start(o_raw[:, :, :], wo[0, :, :, :]).then_inc(ld_o, 16)
            sp.dma_start(gate[:, 0:1], g_xattn.broadcast_to([P, 1])).then_inc(ld_gate, 16)
            sp.dma_start(gate[:, 1:2], g_ffn.broadcast_to([P, 1])).then_inc(ld_gate, 16)
            sp.dma_start(rb_bc[:, :], router_b.broadcast_to([P, NR])).then_inc(ld_small, 16)
            sp.dma_start(emap[:, :], expert_map.broadcast_to([P, NR])).then_inc(ld_small, 16)

            def next_group(g):
                sp.wait_ge(qk_lo_done, 2 * g + 1)
                sp.dma_start(qk_raw[:, 0, :, :, :], wqk[2 * g + 2, :, :, :, :]).then_inc(ld_qk[0], 16)
                sp.wait_ge(wv_lo_done, g + 1)
                sp.dma_start(v_raw[:, :, :], wv[g + 1, :, :, :]).then_inc(ld_wv, 16)
                sp.wait_ge(qk_lo_done, 2 * g + 2)
                sp.dma_start(qk_raw[:, 1, :, :, :], wqk[2 * g + 3, :, :, :, :]).then_inc(ld_qk[1], 16)
                sp.wait_ge(bm_done, 4 * g + 3)
                sp.dma_start(bias_sb[:, 0, :], bias[2 * g + 2, :, :]).then_inc(ld_bias[0], 16)
                sp.wait_ge(bm_done, 4 * g + 4)
                sp.dma_start(bias_sb[:, 1, :], bias[2 * g + 3, :, :]).then_inc(ld_bias[1], 16)
                sp.wait_ge(wo_lo_done, g + 1)
                sp.dma_start(o_raw[:, :, :], wo[g + 1, :, :, :]).then_inc(ld_o, 16)

            next_group(0)
            sp.wait_ge(c_lo_done, 2 * DC)
            sp.dma_start(stage[:, :, :], baseT).then_inc(ld_base, 16)
            with sp.Fori(1, G - 1) as g:
                next_group(g)

            sp.wait_ge(xn_done, B)
            sp.dma_start(row_bc[:, :], base_b.broadcast_to([P, D])).then_inc(ld_bb, 16)
            sp.wait_ge(wv_lo_done, G)
            sp.dma_start(v_raw[:, :, 0:RW], loraR).then_inc(ld_lora, 16)
            sp.wait_ge(qk_lo_done, 2 * G)
            sp.dma_start(x_again[0], x[:, 0:BH, :]).then_inc(ld_x2[0], 16)
            sp.wait_ge(wo_lo_done, G)
            sp.dma_start(o_raw[:, 0, :], lora_B).then_inc(ld_loraB, 16)
            sp.wait_ge(f_w_lo, 3)
            sp.dma_start(x_again[1], x[:, BH:B, :]).then_inc(ld_x2[1], 16)
            for j in range(B):
                sp.wait_ge(f_out, j + 1)
                sp.dma_start(out[:, j, :], out_ring[j % 2]).then_inc(stored[j % 2], 16)
            for done in stored:
                sp.wait_ge(done, 16 * (B // 2))

        @block.gpsimd
        def _(pool):
            pool.memset(ident[:, :], 0.0).then_inc(ident_zero, 1)
            pool.memset(half_neg[:, :], -0.5).then_inc(consts_done, 1)
            pool.iota(eidx[:, :], pattern=[[1, E]], base=0, channel_multiplier=0).then_inc(consts_done, 1)
            pool.wait_ge(ident_zero, 1)
            pool.affine_select(out=ident[:, :], in_=ident[:, :], compare_op=ALU.not_equal, fill=1.0,
                               base=0, pattern=[[-1, P]], channel_multiplier=1).then_inc(ident_done, 1)
            pool.wait_ge(consts_done, 2)

            def split_qk_lo(n, p):
                pool.wait_ge(qk_hi_done, n + 1)
                pool.tensor_tensor(qk_lo[:, p, :, :, :], qk_raw[:, p, :, :, :], f32(qk_hi[:, p, :, :, :]),
                                   ALU.subtract).then_inc(qk_lo_done, 1)

            def split_wv_lo(g):
                pool.wait_ge(wv_hi_done, g + 1)
                pool.tensor_tensor(v_lo[:, :, :], v_raw[:, :, :], f32(v_hi[:, :, :]),
                                   ALU.subtract).then_inc(wv_lo_done, 1)

            def root(h):
                pool.wait_ge(stats_done, 3 * h + 1)
                pool.tensor_tensor(rstd[:, h, :], rstd_in[:, h, :], half_neg[:, :], ALU.pow).then_inc(rstd_done, 1)
                pool.wait_ge(stats_done, 3 * h + 3)
                pool.tensor_tensor(rms_r[:, h, :], rms_in[:, h, :], half_neg[:, :], ALU.pow).then_inc(rms_done, 1)

            def bias_and_mask(g, s):
                t, p, half = 4 * g + s, s % 2, s // 2
                reached(pool, bms_done, t)
                if s < 2:
                    pool.wait_ge(ld_bias[p], 16 * (g + 1))
                if isinstance(g, int) and t == 0:
                    pool.wait_ge(mask_done, 1)
                one = bias_sb[:, p, :].rearrange("p (a k) -> p a k", a=1)
                pool.tensor_tensor(bm[:, :, :], maskneg[:, half * BH:(half + 1) * BH, :],
                                   one.broadcast_to([P, BH, S]), ALU.add).then_inc(bm_done, 1)

            def step(g, s):
                t, first = 4 * g + s, isinstance(g, int) and g == 0
                if not (first and t < 1):
                    reached(pool, s_done, t - 1)
                    pool.wait_ge(small_s_done, t)
                    pool.wait_ge(bm_done, t)
                    pool.tensor_tensor(bms[:, :, :], bm[:, :, :], small_s[:, :, :], ALU.add).then_inc(bms_done, 1)
                if not (first and t < 2):
                    a_remainder(t - 2, ((s - 2) % 4) // 2, s % 2)
                if s == 3 and not (isinstance(g, int) and g == G - 1):
                    split_qk_lo(2 * g + 2, 0)
                if s == 0 and not first:
                    split_qk_lo(2 * g + 1, 1)
                bias_and_mask(g, s)
                if s == 2 and not (isinstance(g, int) and g == G - 1):
                    split_wv_lo(g + 1)

            def a_remainder(u, half, p):
                reached(pool, a_lo_done, u)
                pool.wait_ge(small_a_done, u + 1)
                pool.wait_ge(a_hi_done, u + 1)
                pool.tensor_tensor(a_rest[:, :], small_a[:, :], f32(A_hi[:, half, p, :]),
                                   ALU.subtract).then_inc(a_rest_done, 1)

            root(0)
            split_wv_lo(0)
            split_qk_lo(0, 0)
            split_qk_lo(1, 1)
            step(0, 0)
            for c in range(DC):
                pool.wait_ge(c_hi_done, DC + c + 1)
                pool.tensor_tensor(cT_lo[:, c, rows(1)], stage[:, c, :], f32(cT_hi[:, c, rows(1)]),
                                   ALU.subtract).then_inc(c_lo_done, 1)
            root(1)
            for s in range(1, 4):
                step(0, s)
            with pool.Fori(1, G - 1) as g:
                for s in range(4):
                    step(g, s)
            for s in range(4):
                step(G - 1, s)

            def bms_last():
                reached(pool, s_done, UNITS - 1)
                pool.wait_ge(small_s_done, UNITS)
                pool.wait_ge(bm_done, UNITS)
                pool.tensor_tensor(bms[:, :, :], bm[:, :, :], small_s[:, :, :], ALU.add).then_inc(bms_done, 1)

            def late_low(n, dst, src, hi):
                pool.wait_ge(f_w_hi, n + 1)
                pool.tensor_tensor(dst, src, f32(hi), ALU.subtract).then_inc(f_w_lo, 1)

            def late_root(h):
                pool.wait_ge(f_stat, h + 1)
                pool.tensor_tensor(rstd[:, h, :], rstd_in[:, h, :], half_neg[:, :], ALU.pow).then_inc(f_rstd, 1)

            late_low(0, v_lo[:, :, 0:RW], v_raw[:, :, 0:RW], v_hi[:, :, 0:RW])
            late_low(1, w_base_lo[:, 0:2, :], stage[:, 0:2, :], w_base_hi[:, 0:2, :])
            bms_last()
            late_root(0)
            a_remainder(UNITS - 2, 1, 0)
            late_low(2, w_base_lo[:, 2:4, :], stage[:, 2:4, :], w_base_hi[:, 2:4, :])
            late_low(3, w_loraB_lo, o_raw[:, 0, :], w_loraB_hi)
            a_remainder(UNITS - 1, 1, 1)
            pool.wait_ge(f_tb, 1)
            for j in range(B):
                if j == 2:
                    late_root(1)
                pool.wait_ge(f_x1, j + 1)
                reached(pool, f_out, j - 1)
                if j < 2:
                    pool.wait_ge(exp_done, UNITS)
                    pool.wait_ge(bms_done, UNITS)
                pool.tensor_tensor(x1b[j % 2], acc[:, j, :], row_bc[:, :], ALU.add).then_inc(f_x1b, 1)

        @block.scalar
        def _(act):
            def high(dst, src, done):
                act.activation(dst, src, ACT.Copy).then_inc(done, 1)

            def context_hi(h, c):
                act.wait_ge(ld_c[c if h == 0 else DC], 16)
                high(cT_hi[:, c, rows(h)], stage[:, c, :], c_hi_done)

            def x_hi(j):
                act.wait_ge(xt_psum, j + 1)
                high(xT_hi[:, :, tok(j)], xT_bank[j].rearrange("p (c n) -> p c n", c=DC), x_hi_done)

            def split_qk_hi(g, p):
                act.wait_ge(ld_qk[p], 16 * (g + 1))
                reached(act, k_done, 4 * g - 1 + p)
                high(qk_hi[:, p, :, :, :], qk_raw[:, p, :, :, :], qk_hi_done)

            def split_wv_hi(g):
                act.wait_ge(ld_wv, 16 * (g + 1))
                reached(act, v_done, 4 * g)
                high(v_hi[:, :, :], v_raw[:, :, :], wv_hi_done)

            def split_wo_hi(g):
                act.wait_ge(ld_o, 16 * (g + 1))
                reached(act, o_done, 8 * g)
                high(o_hi[:, :, :], o_raw[:, :, :], wo_hi_done)

            def small_scores(u):
                act.wait_ge(scores_done, u + 1)
                reached(act, bms_done, u)
                act.activation(small_s[:, :, :], Sb[:, :, 1, :], ACT.Copy).then_inc(small_s_done, 1)

            def attention_hi(u, half, p):
                act.wait_ge(pv_done, u + 1)
                reached(act, o_done, out_tiles_before(u, half, p))
                high(A_hi[:, half, p, :].rearrange("p (b q) -> p b q", b=BH), Ab[:, :, 0, :], a_hi_done)
                reached(act, a_rest_done, u)
                act.activation(small_a[:, :].rearrange("p (b q) -> p b q", b=BH), Ab[:, :, 1, :],
                               ACT.Copy).then_inc(small_a_done, 1)

            def exponentials(u):
                act.wait_ge(max_done, u + 1)
                reached(act, norm_done, u)
                for i in range(BH):
                    last = act.activation(p_exp[:, i, :], s_sb[:, i, :], ACT.Exp, bias=negmax[:, i:i + 1],
                                          accum_out=rowsum[:, i:i + 1])
                last.then_inc(exp_done, 1)

            def probs_hi(u):
                act.wait_ge(pt_done, u + 1)
                reached(act, pv_done, u)
                high(P_hl[:, :, 0, :], QP[:, :].rearrange("p (b q) -> p b q", b=BH), p_hi_done)

            def v_piece_hi(v, i):
                act.wait_ge(v_done, v + 1)
                if i == 0:
                    reached(act, pv_done, v - 2)
                if i == 2:
                    reached(act, pv_done, v - 2)
                high(V_hi[:, 2 * i:2 * i + 2, :], Vb[:, :, :], v_hi_done)

            def q_hi(t):
                act.wait_ge(q_done, t + 1)
                reached(act, scores_done, t)
                high(Q_hi[:, :], QP[:, :], q_hi_done)

            def k_hi(t):
                act.wait_ge(k_done, t + 1)
                reached(act, scores_done, t)
                high(K_hl[:, :, 0, :], Kb[:, :].rearrange("p (b k) -> p b k", b=BH), k_hi_done)

            def step(g, s):
                t = 4 * g + s
                first, last = (isinstance(g, int) and g == n for n in (0, G - 1))
                small_scores(t - 1)
                if not (first and t < 2):
                    attention_hi(t - 2, ((s - 2) % 4) // 2, s % 2)
                exponentials(t - 1)
                q_hi(t)
                if last and s == 3:
                    feed_forward_hi(0)
                    feed_forward_hi(1)
                k_hi(t)
                if first and s == 1:
                    x_hi(6)
                if s == 3 and not last:
                    split_qk_hi(g + 1, 0)
                if s == 0:
                    split_qk_hi(g, 1)
                probs_hi(t - 1)
                if not (last and s == 3):
                    v_piece_hi(t + 1, (s + 1) % 4)
                if first and s == 1:
                    x_hi(7)
                if s == 2:
                    if not last:
                        split_wv_hi(g + 1)
                    split_wo_hi(g)

            def feed_forward_hi(n):
                if n == 0:
                    act.wait_ge(ld_lora, 16)
                    act.wait_ge(v_done, UNITS)
                    high(v_hi[:, :, 0:RW], v_raw[:, :, 0:RW], f_w_hi)
                elif n == 1:
                    act.wait_ge(ld_base, 16)
                    act.wait_ge(k_done, UNITS - 1)
                    high(w_base_hi[:, 0:2, :], stage[:, 0:2, :], f_w_hi)
                elif n == 2:
                    act.wait_ge(k_done, UNITS)
                    high(w_base_hi[:, 2:4, :], stage[:, 2:4, :], f_w_hi)
                else:
                    act.wait_ge(ld_loraB, 16)
                    act.wait_ge(pv_done, UNITS - 2)
                    high(w_loraB_hi, o_raw[:, 0, :], f_w_hi)

            for c in range(DC):
                context_hi(0, c)
            split_wv_hi(0)
            split_qk_hi(0, 0)
            v_piece_hi(0, 0)
            k_hi(0)
            x_hi(0)
            x_hi(1)
            split_qk_hi(0, 1)
            v_piece_hi(1, 1)
            x_hi(2)
            x_hi(3)
            for c in range(DC):
                context_hi(1, c)
            q_hi(0)
            x_hi(4)
            x_hi(5)
            for s in range(1, 4):
                step(0, s)
                if s == 1:
                    act.wait_ge(ld_gate, 32)
                    act.activation(tgate[:, :], gate[:, :], ACT.Tanh).then_inc(tanh_done, 1)
            with act.Fori(1, G - 1) as g:
                for s in range(4):
                    step(g, s)
            for s in range(4):
                step(G - 1, s)

            def y_hi(j):
                act.wait_ge(f_yt, j + 1)
                high(xT_hi[:, :, tok(j)], yT_bank[j % 2].rearrange("p (c n) -> p c n", c=DC), f_yhi)

            def route_exp(h):
                act.wait_ge(f_lg, h + 1)
                act.activation(le[:, :, :], lg[:, :, :], ACT.Exp).then_inc(f_exp, 1)

            def hw_hi(h):
                act.wait_ge(f_hwt, h + 1)
                reached(act, f_base, BH * h)
                high(hwT_hi[:, :], Kb[:, :], f_hwhi)

            small_scores(UNITS - 1)
            attention_hi(UNITS - 2, 1, 0)
            feed_forward_hi(2)
            exponentials(UNITS - 1)
            feed_forward_hi(3)
            for j in range(BH):
                y_hi(j)
            probs_hi(UNITS - 1)
            route_exp(0)
            attention_hi(UNITS - 1, 1, 1)
            hw_hi(0)
            for j in range(BH, B):
                y_hi(j)
            route_exp(1)
            hw_hi(1)

        @block.vector
        def _(dve):
            def low(dst, src, hi, done):
                dve.tensor_tensor(dst, src, f32(hi), ALU.subtract).then_inc(done, 1)

            def context_lo(c):
                dve.wait_ge(c_hi_done, c + 1)
                low(cT_lo[:, c, rows(0)], stage[:, c, :], cT_hi[:, c, rows(0)], c_lo_done)

            def layernorm_stats(h):
                for i in range(BH):
                    dve.wait_ge(ld_x[i if h == 0 else BH], 16)
                    dve.bn_stats(bn6[:, h, i, :], acc[:, BH * h + i, :]).then_inc(bn_done, 1)
                for i in range(BH):
                    dve.wait_ge(bn_done, 2 * BH * h + i + 1)
                    dve.bn_aggr(mv[:, h, i, :], bn6[:, h, i, :]).then_inc(bn_done, 1)
                dve.wait_ge(bn_done, 2 * BH * (h + 1))
                dve.tensor_scalar(rstd_in[:, h, :], mv[:, h, :, 1], LN_EPS, None, ALU.add).then_inc(stats_done, 1)

            def rms_stats(h):
                dve.wait_ge(rstd_done, h + 1)
                dve.tensor_tensor(rms_in[:, h, :], mv[:, h, :, 1], rstd[:, h, :], ALU.mult).then_inc(ms_done, 1)
                dve.wait_ge(ms_done, h + 1)
                dve.tensor_tensor(rms_in[:, h, :], rms_in[:, h, :], rstd[:, h, :], ALU.mult).then_inc(stats_done, 1)
                dve.wait_ge(stats_done, 3 * h + 2)
                dve.tensor_scalar(rms_in[:, h, :], rms_in[:, h, :], RMS_EPS, None, ALU.add).then_inc(stats_done, 1)

            def normed(j):
                h, i = j // BH, j % BH
                dve.tensor_scalar(acc[:, j, :], acc[:, j, :], mv[:, h, i, 0:1], rstd[:, h, i:i + 1],
                                  ALU.subtract, ALU.mult).then_inc(hidden_done, 1)
                dve.wait_ge(hidden_done, j + 1)
                if j == 0:
                    dve.wait_ge(ld_lnw, 16)
                if j % BH == 0:
                    dve.wait_ge(rms_done, h + 1)
                reached(dve, xt_psum, j - 1)
                dve.scalar_tensor_tensor(out=xn_ring[j % 2], in0=acc[:, j, :], scalar=rms_r[:, h, i:i + 1],
                                         in1=row_bc[:, :], op0=ALU.mult, op1=ALU.mult).then_inc(xn_done, 1)

            def x_lo(j):
                dve.wait_ge(x_hi_done, j + 1)
                low(xT_lo[:, :, tok(j)], xT_bank[j].rearrange("p (c n) -> p c n", c=DC),
                    xT_hi[:, :, tok(j)], x_lo_done)

            def mask_terms():
                dve.wait_ge(ld_mask, 16)
                dve.tensor_reduce(valid[:, :], mask8, AX.X, ALU.max).then_inc(valid_done, 1)
                dve.tensor_scalar(maskneg[:, :, :], mask8, 1.0, MASKED, ALU.subtract, ALU.mult).then_inc(mask_done, 1)

            def scores(u):
                reached(dve, exp_done, u)
                dve.wait_ge(bms_done, u + 1)
                dve.tensor_tensor(s_sb[:, :, :], Sb[:, :, 0, :], bms[:, :, :], ALU.add).then_inc(s_done, 1)
                dve.wait_ge(s_done, u + 1)
                dve.tensor_reduce(negmax[:, :], s_sb[:, :, :], AX.X, ALU.max, negate=True).then_inc(max_done, 1)

            def attention_lo(u, half, p):
                dve.wait_ge(a_rest_done, u + 1)
                dve.tensor_tensor(A_lo[:, half, p, :].rearrange("p (b q) -> p b q", b=BH), Ab[:, :, 0, :],
                                  a_rest[:, :].rearrange("p (b q) -> p b q", b=BH), ALU.add).then_inc(a_lo_done, 1)

            def normalise(u, half):
                dve.wait_ge(exp_done, u + 1)
                dve.reciprocal(rinv[:, :], rowsum[:, :]).then_inc(rinv_done, 1)
                dve.wait_ge(rinv_done, u + 1)
                dve.tensor_tensor(rscale[:, :], rinv[:, :], valid[:, half * BH:(half + 1) * BH],
                                  ALU.mult).then_inc(rscale_done, 1)
                dve.wait_ge(rscale_done, u + 1)
                reached(dve, pt_done, u)
                scale = rscale[:, :].rearrange("p (b o) -> p b o", o=1).broadcast_to([P, BH, S])
                dve.tensor_tensor(p_norm[:, :, :], p_exp[:, :, :], scale, ALU.mult).then_inc(norm_done, 1)

            def probs_lo(u):
                dve.wait_ge(p_hi_done, u + 1)
                low(P_hl[:, :, 1, :], QP[:, :].rearrange("p (b q) -> p b q", b=BH), P_hl[:, :, 0, :], p_lo_done)

            def v_piece_lo(v, i):
                dve.wait_ge(v_hi_done, v + 1)
                low(V_lo[:, 2 * i:2 * i + 2, :], Vb[:, :, :], V_hi[:, 2 * i:2 * i + 2, :], v_lo_done)

            def add_out(n, j):
                dve.wait_ge(o_done, n + 1)
                bank = late_bank.get(n, Ob[:, :]) if isinstance(n, int) else Ob[:, :]
                dve.tensor_tensor(acc[:, j, :], bank, acc[:, j, :], ALU.add).then_inc(acc_done, 1)

            def q_lo(t):
                dve.wait_ge(q_hi_done, t + 1)
                low(Q_lo[:, :], QP[:, :], Q_hi[:, :], q_lo_done)

            def k_lo(t):
                dve.wait_ge(k_hi_done, t + 1)
                low(K_hl[:, :, 1, :], Kb[:, :].rearrange("p (b k) -> p b k", b=BH), K_hl[:, :, 0, :], k_lo_done)

            def split_wo_lo(g):
                dve.wait_ge(wo_hi_done, g + 1)
                low(o_lo[:, :, :], o_raw[:, :, :], o_hi[:, :, :], wo_lo_done)

            def step(g, s):
                t = 4 * g + s
                first, last = (isinstance(g, int) and g == n for n in (0, G - 1))
                if s == 3:
                    split_wo_lo(g)
                scores(t - 1)
                if not (first and t < 2):
                    attention_lo(t - 2, ((s - 2) % 4) // 2, s % 2)
                if first and s == 1:
                    normed(6)
                normalise(t - 1, ((s - 1) % 4) // 2)
                q_lo(t)
                if last and s == 3:
                    return
                if first and s == 1:
                    x_lo(6)
                    normed(7)
                k_lo(t)
                o, j = t - 3, 2 * ((s - 3) % 4)
                if not (first and t < 3):
                    add_out(2 * o, j)
                probs_lo(t - 1)
                v_piece_lo(t + 1, (s + 1) % 4)
                if not (first and t < 3):
                    add_out(2 * o + 1, j + 1)
                if first and s == 1:
                    x_lo(7)

            layernorm_stats(0)
            context_lo(0)
            context_lo(1)
            rms_stats(0)
            context_lo(2)
            context_lo(3)
            normed(0)
            normed(1)
            x_lo(0)
            v_piece_lo(0, 0)
            normed(2)
            x_lo(1)
            k_lo(0)
            normed(3)
            v_piece_lo(1, 1)
            x_lo(2)
            x_lo(3)
            mask_terms()
            layernorm_stats(1)
            rms_stats(1)
            q_lo(0)
            normed(4)
            normed(5)
            x_lo(4)
            x_lo(5)
            for s in range(1, 4):
                step(0, s)
            with dve.Fori(1, G - 1) as g:
                for s in range(4):
                    step(g, s)
            for s in range(4):
                step(G - 1, s)

            chained = [0]

            def tick(ins):
                chained[0] += 1
                ins.then_inc(f_chain, 1)
                dve.wait_ge(f_chain, chained[0])

            def x1(j):
                h, i = j // BH, j % BH
                dve.wait_ge(acc_done, 2 * UNITS - B + j + 1)
                if i == 0:
                    dve.wait_ge(ld_x2[h], 16)
                    dve.wait_ge(tanh_done, 1)
                dve.scalar_tensor_tensor(out=acc[:, j, :], in0=acc[:, j, :], scalar=tgate[:, 0:1],
                                         in1=x_again[h][:, i, :], op0=ALU.mult, op1=ALU.add).then_inc(f_x1, 1)
                dve.wait_ge(f_x1, j + 1)
                tick(dve.bn_stats(bn6[:, h, i, :], acc[:, j, :]))
                tick(dve.bn_aggr(mv[:, h, i, :], bn6[:, h, i, :]))

            def ffn_rstd_in(h):
                dve.tensor_scalar(rstd_in[:, h, :], mv[:, h, :, 1], LN_EPS, None, ALU.add).then_inc(f_stat, 1)

            def y(j):
                h, i = j // BH, j % BH
                if i == 0:
                    dve.wait_ge(f_rstd, h + 1)
                if j == 0:
                    dve.wait_ge(f_w_lo, 1)
                reached(dve, f_yt, j - 1)
                dve.tensor_scalar(y_ring[j % 2], acc[:, j, :], mv[:, h, i, 0:1], rstd[:, h, i:i + 1],
                                  ALU.subtract, ALU.mult).then_inc(f_y, 1)

            def y_lo(j):
                dve.wait_ge(f_yhi, j + 1)
                low(xT_lo[:, :, tok(j)], yT_bank[j % 2].rearrange("p (c n) -> p c n", c=DC),
                    xT_hi[:, :, tok(j)], f_ylo)

            def router_constants():
                dve.wait_ge(ld_small, 32)
                dve.wait_ge(consts_done, 2)
                tick(dve.tensor_copy(emap_f[:, :], emap[:, :]))
                tick(dve.tensor_copy(eidx_f[:, :], eidx[:, :]))
                for e in range(E):
                    ins = dve.tensor_scalar(onehot[:, e, :], emap_f[:, :], eidx_f[:, e:e + 1], LORA_SCALE,
                                            ALU.is_equal, ALU.mult)
                tick(ins)
                dve.wait_ge(ld_bb, 16)
                dve.wait_ge(tanh_done, 1)
                dve.tensor_scalar(row_bc[:, :], row_bc[:, :], tgate[:, 1:2], None, ALU.mult).then_inc(f_tb, 1)

            def route(h):
                for k in range(2):
                    dve.wait_ge(f_rl, 2 * h + k + 1)
                    bc = rb_bc[:, :].rearrange("p (a n) -> p a n", a=1).broadcast_to([P, 2, NR])
                    tick(dve.tensor_tensor(lg[:, 2 * k:2 * k + 2, :], RL[k][:, :, ER:ER + NR], bc, ALU.add))
                tick(dve.tensor_reduce(lmax[:, :], lg[:, :, :], AX.X, ALU.max))
                top = lmax[:, :].rearrange("p (b o) -> p b o", o=1).broadcast_to([P, BH, NR])
                dve.tensor_tensor(lg[:, :, :], lg[:, :, :], top, ALU.subtract).then_inc(f_lg, 1)
                dve.wait_ge(f_exp, h + 1)
                tick(dve.tensor_reduce(lsum[:, :], le[:, :, :], AX.X, ALU.add))
                tick(dve.reciprocal(lrec[:, :], lsum[:, :]))
                inv = lrec[:, :].rearrange("p (b o) -> p b o", o=1).broadcast_to([P, BH, NR])
                tick(dve.tensor_tensor(probs[:, :, :], le[:, :, :], inv, ALU.mult))
                for i in range(BH):
                    ins = dve.max(top8[:, i, :], probs[:, i, :])
                tick(ins)
                for i in range(BH):
                    ins = dve.match_replace(rest[:, i, :], top8[:, i, :], probs[:, i, :], 0.0)
                tick(ins)
                tick(dve.tensor_tensor(chosen[:, :, :], probs[:, :, :], rest[:, :, :], ALU.subtract))
                sel = chosen[:, :, :].rearrange("p i (a n) -> p i a n", a=1).broadcast_to([P, BH, E, NR])
                one = onehot[:, :, :].rearrange("p (a e) n -> p a e n", a=1).broadcast_to([P, BH, E, NR])
                tick(dve.tensor_tensor(picked[:, :, :, :], sel, one, ALU.mult))
                tick(dve.tensor_reduce(we[:, :, :], picked[:, :, :, :], AX.X, ALU.add))
                reached(dve, f_hwt, h)
                dve.wait_ge(pt_done, UNITS)
                for i in range(BH):
                    w = we[:, i, :].rearrange("p (e o) -> p e o", o=1).broadcast_to([P, E, R])
                    ins = dve.tensor_tensor(hw[:, i, :].rearrange("p (e r) -> p e r", e=E),
                                            RL[i // 2][:, i % 2, 0:ER].rearrange("p (e r) -> p e r", e=E), w, ALU.mult)
                ins.then_inc(f_hw, 1)

            def hw_lo(h):
                dve.wait_ge(f_hwhi, h + 1)
                low(hwT_lo[:, :], Kb[:, :], hwT_hi[:, :], f_hwlo)

            def result(j):
                dve.wait_ge(f_base, j + 1)
                dve.wait_ge(f_x1b, j + 1)
                reached(dve, stored[j % 2], 16 * (j // 2))
                dve.scalar_tensor_tensor(out=out_ring[j % 2], in0=base_bank[j % BH], scalar=tgate[:, 1:2],
                                         in1=x1b[j % 2], op0=ALU.mult, op1=ALU.add).then_inc(f_out, 1)

            add_out(2 * UNITS - 8, 0)
            add_out(2 * UNITS - 7, 1)
            x1(0)
            add_out(2 * UNITS - 6, 2)
            add_out(2 * UNITS - 5, 3)
            x1(1)
            k_lo(UNITS - 1)
            x1(2)
            probs_lo(UNITS - 2)
            x1(3)
            ffn_rstd_in(0)
            scores(UNITS - 1)
            y(0)
            y(1)
            attention_lo(UNITS - 2, 1, 0)
            y_lo(0)
            y(2)
            y_lo(1)
            y(3)
            normalise(UNITS - 1, 1)
            y_lo(2)
            y_lo(3)
            router_constants()
            probs_lo(UNITS - 1)
            route(0)
            attention_lo(UNITS - 1, 1, 1)
            hw_lo(0)
            add_out(2 * UNITS - 4, 4)
            x1(4)
            add_out(2 * UNITS - 3, 5)
            x1(5)
            result(0)
            add_out(2 * UNITS - 2, 6)
            x1(6)
            result(1)
            add_out(2 * UNITS - 1, 7)
            x1(7)
            ffn_rstd_in(1)
            result(2)
            y(4)
            y(5)
            result(3)
            y_lo(4)
            y(6)
            y_lo(5)
            y(7)
            y_lo(6)
            y_lo(7)
            route(1)
            hw_lo(1)
            for j in range(BH, B):
                result(j)

        @block.tensor
        def _(pe):
            def product(dst, w_hi, w_lo, m_hi, m_lo, start, stop):
                pe.matmul(dst, w_lo, m_hi, start=start, stop=False)
                pe.matmul(dst, w_hi, m_lo, start=False, stop=False)
                return pe.matmul(dst, w_hi, m_hi, start=False, stop=stop)

            def x_transpose(j):
                pe.wait_ge(xn_done, j + 1)
                reached(pe, x_lo_done, j if j == 7 else min(j, 6) - 1)
                for c in range(DC):
                    last = pe.transpose(xT_bank[j][:, c * P:(c + 1) * P], xn_ring[j % 2][:, c * P:(c + 1) * P],
                                        ident[:, :])
                last.then_inc(xt_psum, 1)

            def project(bank, p, which, source_hi, source_lo, half, done):
                for c in range(DC):
                    last = product(bank, qk_hi[:, p, which, c, :], qk_lo[:, p, which, c, :],
                                   source_hi[:, c, rows(half)], source_lo[:, c, rows(half)], c == 0, c == DC - 1)
                last.then_inc(done, 1)

            def v_piece(v, g, i):
                reached(pe, v_lo_done, v)
                if i == 0:
                    pe.wait_ge(wv_lo_done, g + 1)
                for k in range(2):
                    j = 2 * i + k
                    for c in range(DC):
                        last = product(Vb[:, k, :], cT_hi[:, c, tok(j)], cT_lo[:, c, tok(j)],
                                       v_hi[:, c, :], v_lo[:, c, :], c == 0, c == DC - 1)
                last.then_inc(v_done, 1)

            def out_tile(n, g, j):
                bank = late_bank.get(n, Ob[:, :]) if isinstance(n, int) else Ob[:, :]
                if isinstance(n, int) and n > 2 * UNITS - 8:
                    pe.wait_ge(acc_done, n - 1)
                else:
                    reached(pe, acc_done, n)
                half, b = j // BH, j % BH
                if j == 0:
                    pe.wait_ge(wo_lo_done, g + 1)
                if j % BH == 0:
                    pe.wait_ge(a_lo_done, 4 * g + 2 * half + 2)
                for p in range(2):
                    last = product(bank, A_hi[:, half, p, tok(b)], A_lo[:, half, p, tok(b)],
                                   o_hi[:, p, :], o_lo[:, p, :], p == 0, p == 1)
                last.then_inc(o_done, 1)

            def transpose_probs(u):
                pe.wait_ge(norm_done, u + 1)
                for b in range(BH):
                    last = pe.transpose(QP[:, tok(b)], p_norm[:, b, :], ident[:, :])
                last.then_inc(pt_done, 1)

            def scores(u):
                pe.wait_ge(q_lo_done, u + 1)
                pe.wait_ge(k_lo_done, u + 1)
                reached(pe, s_done, u)
                reached(pe, small_s_done, u)
                for b in range(BH):
                    pe.matmul(Sb[:, b, :, :], Q_hi[:, tok(b)], K_hl[:, b, :, :], start=True, stop=False)
                    last = pe.matmul(Sb[:, b, 0, :], Q_lo[:, tok(b)], K_hl[:, b, 0, :], start=False, stop=True)
                last.then_inc(scores_done, 1)

            def apply_probs(u, half, p, v_pieces):
                pe.wait_ge(p_lo_done, u + 1)
                pe.wait_ge(v_lo_done, v_pieces)
                reached(pe, a_lo_done, u)
                reached(pe, small_a_done, u)
                for b in range(BH):
                    j, cols = BH * half + b, slice(p * DH, (p + 1) * DH)
                    pe.matmul(Ab[:, b, :, :], V_hi[:, j, cols], P_hl[:, b, :, :], start=True, stop=False)
                    last = pe.matmul(Ab[:, b, 0, :], V_lo[:, j, cols], P_hl[:, b, 0, :], start=False, stop=True)
                last.then_inc(pv_done, 1)

            def q_of(t, g, s):
                if s < 2:
                    pe.wait_ge(qk_lo_done, 2 * g + s % 2 + 1)
                reached(pe, p_lo_done, t - 1)
                project(QP[:, :], s % 2, 0, xT_hi, xT_lo, s // 2, q_done)

            def k_of(t, g, s):
                if s < 2:
                    pe.wait_ge(qk_lo_done, 2 * g + s % 2 + 1)
                reached(pe, k_lo_done, t)
                project(Kb[:, :], s % 2, 1, cT_hi, cT_lo, s // 2, k_done)

            def step(g, s):
                t = 4 * g + s
                first, last = (isinstance(g, int) and g == n for n in (0, G - 1))
                final = last and s == 3
                q_of(t, g, s)
                if final:
                    pe.wait_ge(v_lo_done, UNITS)
                    for j in range(BH):
                        out_tile(2 * UNITS - 8 + j, g, j)
                k_of(t, g, s)
                o, j = t - 3, 2 * ((s - 3) % 4)
                og = g if s == 3 else g - 1
                outs = not final and not (first and t < 3)
                if outs:
                    out_tile(2 * o, og, j)
                if first and s == 1:
                    x_transpose(6)
                    pe.wait_ge(c_lo_done, 2 * DC)
                if not final:
                    v_piece(t + 1, g + (s == 3), (s + 1) % 4)
                pe.wait_ge(q_lo_done, t + 1)
                transpose_probs(t - 1)
                if first and s == 1:
                    x_transpose(7)
                if outs:
                    out_tile(2 * o + 1, og, j + 1)
                scores(t)
                u_half, u_p = ((s - 1) % 4) // 2, (s - 1) % 2
                u_g4 = 4 * (g if s > 0 else g - 1)
                apply_probs(t - 1, u_half, u_p, u_g4 + 2 * u_half + 2)

            pe.wait_ge(c_lo_done, DC)
            v_piece(0, 0, 0)
            k_of(0, 0, 0)
            pe.wait_ge(ident_done, 1)
            x_transpose(0)
            x_transpose(1)
            v_piece(1, 0, 1)
            x_transpose(2)
            x_transpose(3)
            pe.wait_ge(x_lo_done, BH)
            q_of(0, 0, 0)
            x_transpose(4)
            x_transpose(5)
            scores(0)
            step(0, 1)
            pe.wait_ge(x_lo_done, B)
            step(0, 2)
            step(0, 3)
            with pe.Fori(1, G - 1) as g:
                for s in range(4):
                    step(g, s)
            for s in range(4):
                step(G - 1, s)

            def y_transpose(j):
                pe.wait_ge(f_y, j + 1)
                reached(pe, f_ylo, j - 1)
                if j == 0:
                    pe.wait_ge(p_lo_done, UNITS - 1)
                if j == 1:
                    pe.wait_ge(k_lo_done, UNITS)
                if j == BH:
                    pe.wait_ge(acc_done, 2 * UNITS)
                for c in range(DC):
                    last = pe.transpose(yT_bank[j % 2][:, c * P:(c + 1) * P], y_ring[j % 2][:, c * P:(c + 1) * P],
                                        ident[:, :])
                last.then_inc(f_yt, 1)

            def lora_and_router(h):
                pe.wait_ge(f_w_lo, 1)
                reached(pe, f_hw, h)
                if h == 0:
                    pe.wait_ge(acc_done, 2 * UNITS - 4)
                for i in range(BH):
                    j = BH * h + i
                    pe.wait_ge(f_ylo, j + 1)
                    for c in range(DC):
                        last = product(RL[i // 2][:, i % 2, :], xT_hi[:, c, tok(j)], xT_lo[:, c, tok(j)],
                                       v_hi[:, c, 0:RW], v_lo[:, c, 0:RW], c == 0, c == DC - 1)
                    if i % 2:
                        last.then_inc(f_rl, 1)

            def base(j):
                i = j % BH
                pe.wait_ge(f_w_lo, 3)
                if j == 0:
                    pe.wait_ge(s_done, UNITS)
                    pe.wait_ge(small_s_done, UNITS)
                if j == 2:
                    pe.wait_ge(a_lo_done, UNITS)
                reached(pe, f_out, j - BH + 1)
                for c in range(DC):
                    product(base_bank[i], xT_hi[:, c, tok(j)], xT_lo[:, c, tok(j)],
                            w_base_hi[:, c, :], w_base_lo[:, c, :], c == 0, False)

            def hw_transpose(h):
                pe.wait_ge(f_hw, h + 1)
                pe.wait_ge(f_ylo, BH * (h + 1))
                for i in range(BH):
                    last = pe.transpose(Kb[:, tok(i)], hw[:, i, :], ident[:, :])
                last.then_inc(f_hwt, 1)

            def lora_out(j):
                i = j % BH
                pe.wait_ge(f_hwlo, j // BH + 1)
                pe.wait_ge(f_w_lo, 4)
                product(base_bank[i], hwT_hi[:, tok(i)], hwT_lo[:, tok(i)], w_loraB_hi, w_loraB_lo,
                        False, True).then_inc(f_base, 1)

            for j in range(BH):
                y_transpose(j)
            lora_and_router(0)
            pe.wait_ge(f_ylo, BH)
            transpose_probs(UNITS - 1)
            base(0)
            apply_probs(UNITS - 1, 1, 1, UNITS)
            base(1)
            hw_transpose(0)
            pe.wait_ge(p_lo_done, UNITS)
            out_tile(2 * UNITS - 4, G - 1, 4)
            lora_out(0)
            pe.wait_ge(f_hwlo, 1)
            out_tile(2 * UNITS - 3, G - 1, 5)
            lora_out(1)
            out_tile(2 * UNITS - 2, G - 1, 6)
            base(2)
            out_tile(2 * UNITS - 1, G - 1, 7)
            base(3)
            lora_out(2)
            lora_out(3)
            for j in range(BH, B):
                y_transpose(j)
            lora_and_router(1)
            for j in range(BH, B):
                base(j)
            hw_transpose(1)
            for j in range(BH, B):
                lora_out(j)


_INPUTS = ["x", "ctxT", "mask", "g_xattn", "g_ffn", "bias", "lnw", "wqk", "wv", "wo", "baseT", "base_b",
           "loraR", "router_b", "lora_B", "expert_map"]


def kernel(x, ctx_4096, mask_BxSxS2_bk0, g_xattn, g_ffn, L0_xattn_position_bias, L0_xattn_ln_weight,
           L0_xattn_w_q, L0_xattn_w_k, L0_xattn_w_v, L0_xattn_w_out, L0_ffn_base_W, L0_ffn_base_b,
           L0_ffn_router_W, L0_ffn_router_b, L0_ffn_A, L0_ffn_B, L0_ffn_expert_map):
    import numpy as np
    import concourse.bacc as bacc
    from concourse.bass_utils import run_bass_kernel_spmd

    def by_chunk(w):
        return np.asarray(w).reshape(-1, DC, P).transpose(2, 1, 0)

    def heads(w, n):
        return np.asarray(w).reshape(H // n, n * DH, DC, P).transpose(0, 3, 2, 1)

    given = {
        "x": np.asarray(x).transpose(1, 0, 2),
        "ctxT": by_chunk(np.asarray(ctx_4096).reshape(B * S, D)),
        "mask": np.asarray(mask_BxSxS2_bk0).transpose(1, 0, 2),
        "g_xattn": np.asarray(g_xattn).reshape(1, 1),
        "g_ffn": np.asarray(g_ffn).reshape(1, 1),
        "bias": np.asarray(L0_xattn_position_bias),
        "lnw": np.asarray(L0_xattn_ln_weight).reshape(1, D),
        "wqk": np.stack([heads(L0_xattn_w_q, 1), heads(L0_xattn_w_k, 1)], axis=2),
        "wv": heads(L0_xattn_w_v, 2),
        "wo": np.asarray(L0_xattn_w_out).reshape(D, G, 2, DH).transpose(1, 3, 2, 0),
        "baseT": by_chunk(L0_ffn_base_W),
        "base_b": np.asarray(L0_ffn_base_b).reshape(1, D),
        "loraR": np.concatenate([by_chunk(np.asarray(L0_ffn_A).reshape(ER, D)), by_chunk(L0_ffn_router_W),
                                 np.zeros((P, DC, 1), np.float32)], axis=2),
        "router_b": np.asarray(L0_ffn_router_b).reshape(1, NR),
        "lora_B": np.asarray(L0_ffn_B).transpose(0, 2, 1).reshape(ER, D),
        "expert_map": np.asarray(L0_ffn_expert_map).reshape(1, NR),
    }
    given = {name: np.ascontiguousarray(a) for name, a in given.items()}

    nc = bacc.Bacc("TRN2", target_bir_lowering=False, num_devices=1)
    args = [nc.dram_tensor(n, given[n].shape, mybir.dt.from_np(given[n].dtype), kind="ExternalInput").ap()
            for n in _INPUTS]
    args.append(nc.dram_tensor("out", (P, B, D), F32, kind="ExternalOutput").ap())
    build(nc, *args)
    result = run_bass_kernel_spmd(nc, [given], core_ids=[0]).results[0]["out"]
    return result.transpose(1, 0, 2)
```

```python
from contextlib import ExitStack

import concourse.bass as bass
from concourse import mybir

F32 = mybir.dt.float32
F32R = mybir.dt.float32r
U8 = mybir.dt.uint8
I32 = mybir.dt.int32
ALU = mybir.AluOpType
ACT = mybir.ActivationFunctionType
AX = mybir.AxisListType

P = 128
B, S, D = 8, 128, 512
H, DH = 32, 128
DC = D // P
HALVES = 2
BH = B // HALVES
TH = BH * S
G = H // 2
UNITS = 4 * G
NR, E, R = 15, 8, 16
ER = E * R
RW = ER + 16
LN_EPS = 1e-5
RMS_EPS = 1e-5
LORA_SCALE = 2.0
MASKED = 2.0 ** 100


def build(nc, x, ctxT, mask, g_xattn, g_ffn, bias, lnw, wqk, wv, wo, baseT, base_b, loraR, router_b,
          lora_B, expert_map, out):
    with ExitStack() as ctx:
        def sb(name, shape, dt=F32):
            return ctx.enter_context(nc.sbuf_tensor(name, shape, dt))

        def psum(name, shape):
            return ctx.enter_context(nc.psum_tensor(name, shape, F32))

        def sem(name):
            return ctx.enter_context(nc.semaphore(name))

        xT_hi, xT_lo = sb("xT_hi", [P, DC, B * S], F32R), sb("xT_lo", [P, DC, B * S], F32R)
        cT_hi, cT_lo = sb("cT_hi", [P, DC, B * S], F32R), sb("cT_lo", [P, DC, B * S], F32R)
        acc = sb("acc", [P, B, D])
        qk_raw = sb("qk_raw", [P, 2, 2, DC, DH])
        qk_hi, qk_lo = sb("qk_hi", [P, 2, 2, DC, DH], F32R), sb("qk_lo", [P, 2, 2, DC, DH], F32R)
        v_raw = sb("v_raw", [P, DC, 2 * DH])
        v_hi, v_lo = sb("v_hi", [P, DC, 2 * DH], F32R), sb("v_lo", [P, DC, 2 * DH], F32R)
        o_raw = sb("o_raw", [P, 2, D])
        o_hi, o_lo = sb("o_hi", [P, 2, D], F32R), sb("o_lo", [P, 2, D], F32R)
        V_hi, V_lo = sb("V_hi", [P, B, 2 * DH], F32R), sb("V_lo", [P, B, 2 * DH], F32R)
        A_hi, A_lo = sb("A_hi", [P, HALVES, 2, TH], F32R), sb("A_lo", [P, HALVES, 2, TH], F32R)
        Q_hi, Q_lo = sb("Q_hi", [P, TH], F32R), sb("Q_lo", [P, TH], F32R)
        K_hl = sb("K_hl", [P, BH, 2, S], F32R)
        P_hl = sb("P_hl", [P, BH, 2, S], F32R)
        bias_sb = sb("bias_sb", [P, 2, S])
        maskneg = sb("maskneg", [P, B, S])
        bm = sb("bm", [P, BH, S])
        bms = sb("bms", [P, BH, S])
        small_s = sb("small_s", [P, BH, S])
        s_sb = sb("s_sb", [P, BH, S])
        p_exp = sb("p_exp", [P, BH, S])
        p_norm = sb("p_norm", [P, BH, S])
        small_a = sb("small_a", [P, TH])
        a_rest = sb("a_rest", [P, TH])
        stage = sb("stage", [P, DC, D])
        row_bc = sb("row_bc", [P, D])
        ident = sb("ident", [P, P])
        valid = sb("valid", [P, B])
        negmax, rowsum = sb("negmax", [P, BH]), sb("rowsum", [P, BH])
        rinv, rscale = sb("rinv", [P, BH]), sb("rscale", [P, BH])
        gate = sb("gate", [P, 2])
        tgate = sb("tgate", [P, 2])
        half_neg = sb("half_neg", [P, BH])
        bn6 = sb("bn6", [P, 2, BH, 6])
        mv = sb("mv", [P, 2, BH, 2])
        rstd_in, rstd = sb("rstd_in", [P, 2, BH]), sb("rstd", [P, 2, BH])
        rms_in, rms_r = sb("rms_in", [P, 2, BH]), sb("rms_r", [P, 2, BH])
        negmean = sb("negmean", [P, 2, BH])
        norm_scale = sb("norm_scale", [P, 2, BH])
        mask8 = p_norm.ap().rearrange("p a b -> p (a b)")[:, 0:B * S // 4].bitcast(U8)
        mask8 = mask8.rearrange("p (b k) -> p b k", b=B)
        rb_bc = sb("rb_bc", [P, NR])
        emap = sb("emap", [P, NR], I32)
        emap_f = sb("emap_f", [P, NR])
        eidx = sb("eidx", [P, E], I32)
        eidx_f = sb("eidx_f", [P, E])
        onehot = sb("onehot", [P, E, NR])
        lg = sb("lg", [P, BH, NR])
        lmax, lsum, lrec = sb("lmax", [P, BH]), sb("lsum", [P, BH]), sb("lrec", [P, BH])
        le, probs = sb("le", [P, BH, NR]), sb("probs", [P, BH, NR])
        top8 = sb("top8", [P, BH, 8])
        rest = sb("rest", [P, BH, NR])
        chosen = sb("chosen", [P, BH, NR])
        picked = small_s.ap().rearrange("p a b -> p (a b)")[:, 0:BH * E * NR]
        picked = picked.rearrange("p (i e n) -> p i e n", i=BH, e=E)
        we = sb("we", [P, BH, E])

        QP = psum("QP", [P, TH])
        Kb = psum("Kb", [P, TH])
        Vb = psum("Vb", [P, 2, 2 * DH])
        Ob = psum("Ob", [P, D])
        Sb = psum("Sb", [P, BH, 2, S])
        Ab = psum("Ab", [P, BH, 2, S])

        ld_c = [sem(f"ld_c{c}") for c in range(DC)] + [sem("ld_cB")]
        ld_x = [sem(f"ld_x{j}") for j in range(BH)] + [sem("ld_xB")]
        ld_o = sem("ld_o")
        ld_wv = sem("ld_wv")
        ld_qk = [sem("ld_qk0"), sem("ld_qk1")]
        ld_bias = [sem("ld_bias0"), sem("ld_bias1")]
        ld_lnw, ld_mask, ld_gate = sem("ld_lnw"), sem("ld_mask"), sem("ld_gate")
        ld_small, ld_base, ld_lora, ld_loraB = sem("ld_small"), sem("ld_base"), sem("ld_lora"), sem("ld_loraB")
        ld_x2 = [sem("ld_x2A"), sem("ld_x2B")]
        ld_bb = sem("ld_bb")
        stored = [sem("stored0"), sem("stored1")]
        ident_zero, ident_done, consts_done = sem("ident_zero"), sem("ident_done"), sem("consts_done")
        c_hi_done, c_lo_done = sem("c_hi_done"), sem("c_lo_done")
        stats_done = sem("stats_done")
        rstd_done, rms_done = sem("rstd_done"), sem("rms_done")
        mean_done, scale_done = sem("mean_done"), sem("scale_done")
        centred_done, xn_done, hidden_done = (sem(n) for n in (
            "centred_done", "xn_done", "hidden_done"))
        xt_psum, x_hi_done, x_lo_done = sem("xt_psum"), sem("x_hi_done"), sem("x_lo_done")
        tanh_done, mask_done, valid_done = sem("tanh_done"), sem("mask_done"), sem("valid_done")
        bn_done, ms_done = sem("bn_done"), sem("ms_done")
        qk_hi_done, qk_lo_done = sem("qk_hi_done"), sem("qk_lo_done")
        wv_hi_done, wv_lo_done = sem("wv_hi_done"), sem("wv_lo_done")
        wo_hi_done, wo_lo_done = sem("wo_hi_done"), sem("wo_lo_done")
        q_done, k_done, scores_done, pt_done, pv_done = (sem(n) for n in (
            "q_done", "k_done", "scores_done", "pt_done", "pv_done"))
        q_hi_done, k_hi_done, p_hi_done, a_hi_done = (sem(n) for n in (
            "q_hi_done", "k_hi_done", "p_hi_done", "a_hi_done"))
        q_lo_done, k_lo_done, p_lo_done, a_lo_done = (sem(n) for n in (
            "q_lo_done", "k_lo_done", "p_lo_done", "a_lo_done"))
        small_s_done, small_a_done, exp_done = sem("small_s_done"), sem("small_a_done"), sem("exp_done")
        bm_done, bms_done, a_rest_done = sem("bm_done"), sem("bms_done"), sem("a_rest_done")
        s_done, max_done, rinv_done, rscale_done, norm_done = (sem(n) for n in (
            "s_done", "max_done", "rinv_done", "rscale_done", "norm_done"))
        v_done, v_hi_done, v_lo_done = sem("v_done"), sem("v_hi_done"), sem("v_lo_done")
        o_done, acc_done = sem("o_done"), sem("acc_done")
        f_w_hi, f_w_lo = sem("f_w_hi"), sem("f_w_lo")
        f_u, f_x1, f_bn, f_mv = sem("f_u"), sem("f_x1"), sem("f_bn"), sem("f_mv")
        f_stat, f_rstd, f_y = sem("f_stat"), sem("f_rstd"), sem("f_y")
        f_yt, f_yhi, f_ylo = sem("f_yt"), sem("f_yhi"), sem("f_ylo")
        f_rl, f_lg, f_chain, f_exp = sem("f_rl"), sem("f_lg"), sem("f_chain"), sem("f_exp")
        f_hw, f_hwt, f_hwhi, f_hwlo = sem("f_hw"), sem("f_hwt"), sem("f_hwhi"), sem("f_hwlo")
        f_base, f_x1b, f_out, f_tb = sem("f_base"), sem("f_x1b"), sem("f_out"), sem("f_tb")

        block = ctx.enter_context(nc.Block())

        def reached(eng, s, n):
            if not isinstance(n, int) or n > 0:
                eng.wait_ge(s, n)

        def f32(ap):
            return ap.bitcast(F32)

        def rows(half):
            return slice(half * TH, (half + 1) * TH)

        def tok(j):
            return slice(j * S, (j + 1) * S)

        def flat(t):
            names = "abcd"[:len(t.shape) - 1]
            return t.ap().rearrange(f"p {' '.join(names)} -> p ({' '.join(names)})")

        w_base_hi = flat(qk_hi).rearrange("p (c n) -> p c n", c=DC)
        w_base_lo = flat(qk_lo).rearrange("p (c n) -> p c n", c=DC)
        x_again = flat(qk_raw).rearrange("p (i n) -> p i n", i=BH)
        y_ring = [flat(v_raw)[:, 0:D], flat(v_raw)[:, D:2 * D]]
        xn_at = [small_a[:, :], a_rest[:, :], flat(s_sb), flat(p_exp)]
        w_loraB_hi = V_hi[:, 0:2, :].rearrange("p a b -> p (a b)")
        w_loraB_lo = V_lo[:, 0:2, :].rearrange("p a b -> p (a b)")
        yT_bank = [QP[:, :], Kb[:, :]]
        RL = [flat(Vb)[:, 0:2 * RW].rearrange("p (i n) -> p i n", i=2),
              Ob[:, 0:2 * RW].rearrange("p (i n) -> p i n", i=2)]
        base_bank = [flat(bank)[:, k * D:(k + 1) * D] for bank in (Sb, Ab) for k in range(2)]
        xT_bank = 2 * (base_bank[2:] + [Ob[:, :], base_bank[0]])
        xT_bank[7] = base_bank[2]
        V_bank1 = base_bank[1].rearrange("p (a b) -> p a b", a=2)
        late_banks = 2 * [Ob[:, :], flat(Vb)] + 2 * [QP[:, :], Kb[:, :]]
        late_bank = {2 * UNITS - B + j: bank for j, bank in enumerate(late_banks)}
        hw = p_norm
        hwT_hi, hwT_lo = Q_hi, Q_lo
        x1b = [flat(s_sb), flat(bm)]
        out_ring = [flat(p_exp), flat(bms)]

        @block.sync
        def _(sp):
            sp.dma_start(v_raw[:, :, :], wv[0, :, :, :]).then_inc(ld_wv, 16)
            for c in range(DC):
                sp.dma_start(stage[:, c, :], ctxT[:, c, rows(0)]).then_inc(ld_c[c], 16)
            for j in range(BH):
                sp.dma_start(acc[:, j, :], x[:, j, :]).then_inc(ld_x[j], 16)
            sp.dma_start(mask8, mask).then_inc(ld_mask, 16)
            sp.dma_start(qk_raw[:, 0, :, :, :], wqk[0, :, :, :, :]).then_inc(ld_qk[0], 16)
            sp.dma_start(row_bc[:, :], lnw.broadcast_to([P, D])).then_inc(ld_lnw, 16)
            sp.dma_start(qk_raw[:, 1, :, :, :], wqk[1, :, :, :, :]).then_inc(ld_qk[1], 16)
            sp.dma_start(bias_sb[:, 0, :], bias[0, :, :]).then_inc(ld_bias[0], 16)
            sp.dma_start(acc[:, BH:B, :], x[:, BH:B, :]).then_inc(ld_x[BH], 16)
            sp.wait_ge(c_lo_done, DC)
            sp.dma_start(stage[:, :, :], ctxT[:, :, rows(1)]).then_inc(ld_c[DC], 16)
            sp.dma_start(bias_sb[:, 1, :], bias[1, :, :]).then_inc(ld_bias[1], 16)
            sp.dma_start(o_raw[:, :, :], wo[0, :, :, :]).then_inc(ld_o, 16)
            sp.dma_start(gate[:, 0:1], g_xattn.broadcast_to([P, 1])).then_inc(ld_gate, 16)
            sp.dma_start(gate[:, 1:2], g_ffn.broadcast_to([P, 1])).then_inc(ld_gate, 16)
            sp.dma_start(rb_bc[:, :], router_b.broadcast_to([P, NR])).then_inc(ld_small, 16)
            sp.dma_start(emap[:, :], expert_map.broadcast_to([P, NR])).then_inc(ld_small, 16)

            def next_group(g):
                sp.wait_ge(qk_lo_done, 2 * g + 1)
                sp.dma_start(qk_raw[:, 0, :, :, :], wqk[2 * g + 2, :, :, :, :]).then_inc(ld_qk[0], 16)
                sp.wait_ge(wv_lo_done, g + 1)
                sp.dma_start(v_raw[:, :, :], wv[g + 1, :, :, :]).then_inc(ld_wv, 16)
                sp.wait_ge(qk_lo_done, 2 * g + 2)
                sp.dma_start(qk_raw[:, 1, :, :, :], wqk[2 * g + 3, :, :, :, :]).then_inc(ld_qk[1], 16)
                sp.wait_ge(bm_done, 4 * g + 3)
                sp.dma_start(bias_sb[:, 0, :], bias[2 * g + 2, :, :]).then_inc(ld_bias[0], 16)
                sp.wait_ge(bm_done, 4 * g + 4)
                sp.dma_start(bias_sb[:, 1, :], bias[2 * g + 3, :, :]).then_inc(ld_bias[1], 16)
                sp.wait_ge(wo_lo_done, g + 1)
                sp.dma_start(o_raw[:, :, :], wo[g + 1, :, :, :]).then_inc(ld_o, 16)

            sp.wait_ge(xn_done, B)
            sp.dma_start(row_bc[:, :], base_b.broadcast_to([P, D])).then_inc(ld_bb, 16)
            next_group(0)
            sp.wait_ge(c_lo_done, 2 * DC)
            sp.dma_start(stage[:, :, :], baseT).then_inc(ld_base, 16)
            with sp.Fori(1, G - 1) as g:
                next_group(g)

            sp.wait_ge(wv_lo_done, G)
            sp.dma_start(v_raw[:, :, 0:RW], loraR).then_inc(ld_lora, 16)
            sp.wait_ge(qk_lo_done, 2 * G)
            sp.dma_start(x_again, x[:, 0:BH, :]).then_inc(ld_x2[0], 16)
            sp.wait_ge(wo_lo_done, G)
            sp.dma_start(o_raw[:, 0, :], lora_B).then_inc(ld_loraB, 16)
            sp.wait_ge(f_u, BH)
            sp.dma_start(x_again, x[:, BH:B, :]).then_inc(ld_x2[1], 16)
            for j in range(B):
                sp.wait_ge(f_out, j + 1)
                sp.dma_start(out[:, j, :], out_ring[j % 2]).then_inc(stored[j % 2], 16)
            for done in stored:
                sp.wait_ge(done, 16 * (B // 2))

        @block.gpsimd
        def _(pool):
            pool.memset(ident[:, :], 0.0).then_inc(ident_zero, 1)
            pool.memset(half_neg[:, :], -0.5).then_inc(consts_done, 1)
            pool.iota(eidx[:, :], pattern=[[1, E]], base=0, channel_multiplier=0).then_inc(consts_done, 1)
            pool.wait_ge(ident_zero, 1)
            pool.affine_select(out=ident[:, :], in_=ident[:, :], compare_op=ALU.not_equal, fill=1.0,
                               base=0, pattern=[[-1, P]], channel_multiplier=1).then_inc(ident_done, 1)
            pool.wait_ge(consts_done, 2)

            def split_qk_lo(n, p):
                pool.wait_ge(qk_hi_done, n + 1)
                pool.tensor_tensor(qk_lo[:, p, :, :, :], qk_raw[:, p, :, :, :], f32(qk_hi[:, p, :, :, :]),
                                   ALU.subtract).then_inc(qk_lo_done, 1)

            def split_wv_lo(g):
                pool.wait_ge(wv_hi_done, g + 1)
                pool.tensor_tensor(v_lo[:, :, :], v_raw[:, :, :], f32(v_hi[:, :, :]),
                                   ALU.subtract).then_inc(wv_lo_done, 1)

            def root(h):
                pool.wait_ge(stats_done, 3 * h + 1)
                pool.tensor_tensor(rstd[:, h, :], rstd_in[:, h, :], half_neg[:, :], ALU.pow).then_inc(rstd_done, 1)
                pool.wait_ge(stats_done, 3 * h + 3)
                pool.tensor_tensor(rms_r[:, h, :], rms_in[:, h, :], half_neg[:, :], ALU.pow).then_inc(rms_done, 1)

            def bias_and_mask(g, s):
                t, p, half = 4 * g + s, s % 2, s // 2
                reached(pool, bms_done, t)
                if s < 2:
                    pool.wait_ge(ld_bias[p], 16 * (g + 1))
                if isinstance(g, int) and t == 0:
                    pool.wait_ge(mask_done, 1)
                one = bias_sb[:, p, :].rearrange("p (a k) -> p a k", a=1)
                pool.tensor_tensor(bm[:, :, :], maskneg[:, half * BH:(half + 1) * BH, :],
                                   one.broadcast_to([P, BH, S]), ALU.add).then_inc(bm_done, 1)

            def step(g, s):
                t, first = 4 * g + s, isinstance(g, int) and g == 0
                if not (first and t < 1):
                    reached(pool, s_done, t - 1)
                    pool.wait_ge(small_s_done, t)
                    pool.wait_ge(bm_done, t)
                    pool.tensor_tensor(bms[:, :, :], bm[:, :, :], small_s[:, :, :], ALU.add).then_inc(bms_done, 1)
                if not (first and t < 2):
                    a_remainder(t - 2, ((s - 2) % 4) // 2, s % 2)
                if s == 3 and not (isinstance(g, int) and g == G - 1):
                    split_qk_lo(2 * g + 2, 0)
                if s == 0 and not first:
                    split_qk_lo(2 * g + 1, 1)
                bias_and_mask(g, s)
                if s == 2 and not (isinstance(g, int) and g == G - 1):
                    split_wv_lo(g + 1)

            def a_remainder(u, half, p):
                reached(pool, a_lo_done, u)
                pool.wait_ge(small_a_done, u + 1)
                pool.wait_ge(a_hi_done, u + 1)
                pool.tensor_tensor(a_rest[:, :], small_a[:, :], f32(A_hi[:, half, p, :]),
                                   ALU.subtract).then_inc(a_rest_done, 1)

            def context_lo(c):
                pool.wait_ge(c_hi_done, DC + c + 1)
                pool.tensor_tensor(cT_lo[:, c, rows(1)], stage[:, c, :], f32(cT_hi[:, c, rows(1)]),
                                   ALU.subtract).then_inc(c_lo_done, 1)

            split_wv_lo(0)
            root(0)
            split_qk_lo(0, 0)
            split_qk_lo(1, 1)
            step(0, 0)
            context_lo(0)
            root(1)
            context_lo(1)
            for s in range(1, 4):
                step(0, s)
            with pool.Fori(1, G - 1) as g:
                for s in range(4):
                    step(g, s)
            for s in range(4):
                step(G - 1, s)

            def bms_last():
                reached(pool, s_done, UNITS - 1)
                pool.wait_ge(small_s_done, UNITS)
                pool.wait_ge(bm_done, UNITS)
                pool.tensor_tensor(bms[:, :, :], bm[:, :, :], small_s[:, :, :], ALU.add).then_inc(bms_done, 1)

            def late_low(n, dst, src, hi):
                pool.wait_ge(f_w_hi, n + 1)
                pool.tensor_tensor(dst, src, f32(hi), ALU.subtract).then_inc(f_w_lo, 1)

            def late_root(r):
                h, pair = r // 2, slice(2 * (r % 2), 2 * (r % 2) + 2)
                pool.wait_ge(f_stat, r + 1)
                pool.tensor_tensor(rstd[:, h, pair], rstd_in[:, h, pair], half_neg[:, 0:2], ALU.pow).then_inc(f_rstd, 1)

            late_low(0, v_lo[:, :, 0:RW], v_raw[:, :, 0:RW], v_hi[:, :, 0:RW])
            late_low(1, w_base_lo[:, 0:2, :], stage[:, 0:2, :], w_base_hi[:, 0:2, :])
            late_root(0)
            bms_last()
            late_root(1)
            a_remainder(UNITS - 2, 1, 0)
            late_low(2, w_base_lo[:, 2:4, :], stage[:, 2:4, :], w_base_hi[:, 2:4, :])
            late_low(3, w_loraB_lo, o_raw[:, 0, :], w_loraB_hi)
            a_remainder(UNITS - 1, 1, 1)
            pool.wait_ge(f_tb, 1)
            for j in range(B):
                if j == 2:
                    late_root(2)
                    late_root(3)
                pool.wait_ge(f_x1, j + 1)
                reached(pool, f_out, j - 1)
                if j < 2:
                    pool.wait_ge(exp_done, UNITS)
                    pool.wait_ge(bms_done, UNITS)
                pool.tensor_tensor(x1b[j % 2], acc[:, j, :], row_bc[:, :], ALU.add).then_inc(f_x1b, 1)

        @block.scalar
        def _(act):
            def high(dst, src, done):
                act.activation(dst, src, ACT.Copy).then_inc(done, 1)

            def context_hi(h, c):
                act.wait_ge(ld_c[c if h == 0 else DC], 16)
                high(cT_hi[:, c, rows(h)], stage[:, c, :], c_hi_done)

            def centred(j):
                h, i = j // BH, j % BH
                act.wait_ge(mean_done, h + 1)
                act.activation(acc[:, j, :], acc[:, j, :], ACT.Identity,
                               bias=negmean[:, h, i:i + 1]).then_inc(centred_done, 1)

            def hidden(j):
                h, i = j // BH, j % BH
                act.wait_ge(rstd_done, h + 1)
                act.wait_ge(xn_done, j + 1)
                act.activation(acc[:, j, :], acc[:, j, :], ACT.Identity,
                               scale=rstd[:, h, i:i + 1]).then_inc(hidden_done, 1)

            def x_hi(j):
                act.wait_ge(xt_psum, j + 1)
                high(xT_hi[:, :, tok(j)], xT_bank[j].rearrange("p (c n) -> p c n", c=DC), x_hi_done)

            def split_qk_hi(g, p):
                act.wait_ge(ld_qk[p], 16 * (g + 1))
                reached(act, k_done, 4 * g - 1 + p)
                high(qk_hi[:, p, :, :, :], qk_raw[:, p, :, :, :], qk_hi_done)

            def split_wv_hi(g):
                act.wait_ge(ld_wv, 16 * (g + 1))
                reached(act, v_done, 4 * g)
                high(v_hi[:, :, :], v_raw[:, :, :], wv_hi_done)

            def split_wo_hi(g):
                act.wait_ge(ld_o, 16 * (g + 1))
                reached(act, o_done, 8 * g)
                high(o_hi[:, :, :], o_raw[:, :, :], wo_hi_done)

            def small_scores(u):
                act.wait_ge(scores_done, u + 1)
                reached(act, bms_done, u)
                act.activation(small_s[:, :, :], Sb[:, :, 1, :], ACT.Copy).then_inc(small_s_done, 1)

            def attention_hi(u, half, p):
                act.wait_ge(pv_done, u + 1)
                high(A_hi[:, half, p, :].rearrange("p (b q) -> p b q", b=BH), Ab[:, :, 0, :], a_hi_done)
                reached(act, a_rest_done, u)
                act.activation(small_a[:, :].rearrange("p (b q) -> p b q", b=BH), Ab[:, :, 1, :],
                               ACT.Copy).then_inc(small_a_done, 1)

            def exponentials(u):
                act.wait_ge(max_done, u + 1)
                reached(act, norm_done, u)
                for i in range(BH):
                    last = act.activation(p_exp[:, i, :], s_sb[:, i, :], ACT.Exp, bias=negmax[:, i:i + 1],
                                          accum_out=rowsum[:, i:i + 1])
                last.then_inc(exp_done, 1)

            def probs_hi(u):
                act.wait_ge(pt_done, u + 1)
                reached(act, pv_done, u)
                high(P_hl[:, :, 0, :], QP[:, :].rearrange("p (b q) -> p b q", b=BH), p_hi_done)

            def v_piece_hi(v, i):
                act.wait_ge(v_done, v + 1)
                if i == 0:
                    reached(act, pv_done, v - 2)
                if i == 2:
                    reached(act, pv_done, v - 2)
                bank = V_bank1 if isinstance(v, int) and v == 1 else Vb[:, :, :]
                high(V_hi[:, 2 * i:2 * i + 2, :], bank, v_hi_done)

            def q_hi(t):
                act.wait_ge(q_done, t + 1)
                reached(act, scores_done, t)
                high(Q_hi[:, :], QP[:, :], q_hi_done)

            def k_hi(t):
                act.wait_ge(k_done, t + 1)
                reached(act, scores_done, t)
                high(K_hl[:, :, 0, :], Kb[:, :].rearrange("p (b k) -> p b k", b=BH), k_hi_done)

            def step(g, s):
                t = 4 * g + s
                first, last = (isinstance(g, int) and g == n for n in (0, G - 1))
                small_scores(t - 1)
                if first and s == 1:
                    k_hi(t)
                    q_hi(t)
                    for j in range(BH, B):
                        x_hi(j)
                    exponentials(t - 1)
                else:
                    attention_hi(t - 2, ((s - 2) % 4) // 2, s % 2)
                    exponentials(t - 1)
                    q_hi(t)
                if last and s == 3:
                    feed_forward_hi(0)
                    feed_forward_hi(1)
                if not (first and s == 1):
                    k_hi(t)
                if first and s < 3:
                    hidden(BH + 2 * s - 2)
                    hidden(BH + 2 * s - 1)
                if s == 3 and not last:
                    split_qk_hi(g + 1, 0)
                if s == 0:
                    split_qk_hi(g, 1)
                probs_hi(t - 1)
                if not (last and s == 3):
                    v_piece_hi(t + 1, (s + 1) % 4)
                if s == 2:
                    if not last:
                        split_wv_hi(g + 1)
                    split_wo_hi(g)

            def feed_forward_hi(n):
                if n == 0:
                    act.wait_ge(ld_lora, 16)
                    act.wait_ge(v_done, UNITS)
                    high(v_hi[:, :, 0:RW], v_raw[:, :, 0:RW], f_w_hi)
                elif n == 1:
                    act.wait_ge(ld_base, 16)
                    act.wait_ge(k_done, UNITS - 1)
                    high(w_base_hi[:, 0:2, :], stage[:, 0:2, :], f_w_hi)
                elif n == 2:
                    act.wait_ge(k_done, UNITS)
                    high(w_base_hi[:, 2:4, :], stage[:, 2:4, :], f_w_hi)
                else:
                    act.wait_ge(ld_loraB, 16)
                    act.wait_ge(pv_done, UNITS - 2)
                    high(w_loraB_hi, o_raw[:, 0, :], f_w_hi)

            split_wv_hi(0)
            for c in range(DC):
                context_hi(0, c)
            centred(0)
            split_qk_hi(0, 0)
            centred(1)
            v_piece_hi(0, 0)
            centred(2)
            centred(3)
            split_qk_hi(0, 1)
            v_piece_hi(1, 1)
            for j in range(BH):
                x_hi(j)
            hidden(0)
            hidden(1)
            hidden(2)
            k_hi(0)
            for c in range(DC):
                context_hi(1, c)
            q_hi(0)
            hidden(3)
            for j in range(BH, B):
                centred(j)
            for s in range(1, 4):
                step(0, s)
                if s == 1:
                    act.wait_ge(ld_gate, 32)
                    act.activation(tgate[:, :], gate[:, :], ACT.Tanh).then_inc(tanh_done, 1)
            with act.Fori(1, G - 1) as g:
                for s in range(4):
                    step(g, s)
            for s in range(4):
                step(G - 1, s)

            def y_hi(j):
                act.wait_ge(f_yt, j + 1)
                high(xT_hi[:, :, tok(j)], yT_bank[j % 2].rearrange("p (c n) -> p c n", c=DC), f_yhi)

            def route_exp(h):
                act.wait_ge(f_lg, h + 1)
                act.activation(le[:, :, :], lg[:, :, :], ACT.Exp).then_inc(f_exp, 1)

            def hw_hi(h):
                act.wait_ge(f_hwt, h + 1)
                reached(act, f_base, BH * h)
                high(hwT_hi[:, :], Kb[:, :], f_hwhi)

            small_scores(UNITS - 1)
            feed_forward_hi(2)
            y_hi(0)
            y_hi(1)
            attention_hi(UNITS - 2, 1, 0)
            exponentials(UNITS - 1)
            y_hi(2)
            y_hi(3)
            feed_forward_hi(3)
            probs_hi(UNITS - 1)
            route_exp(0)
            attention_hi(UNITS - 1, 1, 1)
            hw_hi(0)
            for j in range(BH, B):
                y_hi(j)
            route_exp(1)
            hw_hi(1)

        @block.vector
        def _(dve):
            def low(dst, src, hi, done):
                dve.tensor_tensor(dst, src, f32(hi), ALU.subtract).then_inc(done, 1)

            def context_lo(h, c):
                dve.wait_ge(c_hi_done, DC * h + c + 1)
                low(cT_lo[:, c, rows(h)], stage[:, c, :], cT_hi[:, c, rows(h)], c_lo_done)

            def layernorm_stats(h):
                for i in range(BH):
                    dve.wait_ge(ld_x[i if h == 0 else BH], 16)
                    dve.bn_stats(bn6[:, h, i, :], acc[:, BH * h + i, :]).then_inc(bn_done, 1)
                for i in range(BH):
                    dve.wait_ge(bn_done, 2 * BH * h + i + 1)
                    dve.bn_aggr(mv[:, h, i, :], bn6[:, h, i, :]).then_inc(bn_done, 1)
                dve.wait_ge(bn_done, 2 * BH * (h + 1))
                dve.tensor_scalar(rstd_in[:, h, :], mv[:, h, :, 1], LN_EPS, None, ALU.add).then_inc(stats_done, 1)
                dve.tensor_scalar(negmean[:, h, :], mv[:, h, :, 0], -1.0, None, ALU.mult).then_inc(mean_done, 1)

            def rms_stats(h):
                dve.wait_ge(rstd_done, h + 1)
                dve.tensor_tensor(rms_in[:, h, :], mv[:, h, :, 1], rstd[:, h, :], ALU.mult).then_inc(ms_done, 1)
                dve.wait_ge(ms_done, h + 1)
                dve.tensor_tensor(rms_in[:, h, :], rms_in[:, h, :], rstd[:, h, :], ALU.mult).then_inc(stats_done, 1)
                dve.wait_ge(stats_done, 3 * h + 2)
                dve.tensor_scalar(rms_in[:, h, :], rms_in[:, h, :], RMS_EPS, None, ALU.add).then_inc(stats_done, 1)

            def norm_scales(h):
                dve.wait_ge(rms_done, h + 1)
                dve.tensor_tensor(norm_scale[:, h, :], rstd[:, h, :], rms_r[:, h, :], ALU.mult).then_inc(scale_done, 1)

            def normed(j):
                h, i = j // BH, j % BH
                if j == 0:
                    dve.wait_ge(ld_lnw, 16)
                if i == 0:
                    dve.wait_ge(scale_done, h + 1)
                dve.wait_ge(centred_done, j + 1)
                if j >= BH:
                    dve.wait_ge(xt_psum, j - BH + 1)
                dve.scalar_tensor_tensor(out=xn_at[j % BH], in0=acc[:, j, :], scalar=norm_scale[:, h, i:i + 1],
                                         in1=row_bc[:, :], op0=ALU.mult, op1=ALU.mult).then_inc(xn_done, 1)

            def x_lo(j):
                dve.wait_ge(x_hi_done, j + 1)
                low(xT_lo[:, :, tok(j)], xT_bank[j].rearrange("p (c n) -> p c n", c=DC),
                    xT_hi[:, :, tok(j)], x_lo_done)

            def mask_valid():
                dve.wait_ge(ld_mask, 16)
                dve.tensor_reduce(valid[:, :], mask8, AX.X, ALU.max).then_inc(valid_done, 1)

            def mask_negative():
                dve.tensor_scalar(maskneg[:, :, :], mask8, 1.0, MASKED, ALU.subtract, ALU.mult).then_inc(mask_done, 1)

            def scores(u):
                reached(dve, exp_done, u)
                dve.wait_ge(bms_done, u + 1)
                dve.tensor_tensor(s_sb[:, :, :], Sb[:, :, 0, :], bms[:, :, :], ALU.add).then_inc(s_done, 1)
                dve.wait_ge(s_done, u + 1)
                dve.tensor_reduce(negmax[:, :], s_sb[:, :, :], AX.X, ALU.max, negate=True).then_inc(max_done, 1)

            def attention_lo(u, half, p):
                dve.wait_ge(a_rest_done, u + 1)
                dve.tensor_tensor(A_lo[:, half, p, :].rearrange("p (b q) -> p b q", b=BH), Ab[:, :, 0, :],
                                  a_rest[:, :].rearrange("p (b q) -> p b q", b=BH), ALU.add).then_inc(a_lo_done, 1)

            def normalise(u, half):
                dve.wait_ge(exp_done, u + 1)
                dve.reciprocal(rinv[:, :], rowsum[:, :]).then_inc(rinv_done, 1)
                dve.wait_ge(rinv_done, u + 1)
                dve.tensor_tensor(rscale[:, :], rinv[:, :], valid[:, half * BH:(half + 1) * BH],
                                  ALU.mult).then_inc(rscale_done, 1)
                dve.wait_ge(rscale_done, u + 1)
                reached(dve, pt_done, u)
                scale = rscale[:, :].rearrange("p (b o) -> p b o", o=1).broadcast_to([P, BH, S])
                dve.tensor_tensor(p_norm[:, :, :], p_exp[:, :, :], scale, ALU.mult).then_inc(norm_done, 1)

            def probs_lo(u):
                dve.wait_ge(p_hi_done, u + 1)
                low(P_hl[:, :, 1, :], QP[:, :].rearrange("p (b q) -> p b q", b=BH), P_hl[:, :, 0, :], p_lo_done)

            def v_piece_lo(v, i):
                dve.wait_ge(v_hi_done, v + 1)
                bank = V_bank1 if isinstance(v, int) and v == 1 else Vb[:, :, :]
                low(V_lo[:, 2 * i:2 * i + 2, :], bank, V_hi[:, 2 * i:2 * i + 2, :], v_lo_done)

            def add_out(n, j):
                dve.wait_ge(o_done, n + 1)
                dve.tensor_tensor(acc[:, j, :], Ob[:, :], acc[:, j, :], ALU.add).then_inc(acc_done, 1)

            def q_lo(t):
                dve.wait_ge(q_hi_done, t + 1)
                low(Q_lo[:, :], QP[:, :], Q_hi[:, :], q_lo_done)

            def k_lo(t):
                dve.wait_ge(k_hi_done, t + 1)
                low(K_hl[:, :, 1, :], Kb[:, :].rearrange("p (b k) -> p b k", b=BH), K_hl[:, :, 0, :], k_lo_done)

            def split_wo_lo(g):
                dve.wait_ge(wo_hi_done, g + 1)
                low(o_lo[:, :, :], o_raw[:, :, :], o_hi[:, :, :], wo_lo_done)

            def step(g, s):
                t = 4 * g + s
                first, last = (isinstance(g, int) and g == n for n in (0, G - 1))
                if first and s == 3:
                    dve.wait_ge(hidden_done, B)
                if s == 3:
                    split_wo_lo(g)
                if first and s == 1:
                    x_lo(4)
                    dve.wait_ge(xt_psum, 7)
                scores(t - 1)
                if not (first and t < 2):
                    attention_lo(t - 2, ((s - 2) % 4) // 2, s % 2)
                if first and s == 1:
                    q_lo(t)
                    x_lo(5)
                    x_lo(6)
                normalise(t - 1, ((s - 1) % 4) // 2)
                if not (first and s == 1):
                    q_lo(t)
                if last and s == 3:
                    return
                k_lo(t)
                if first and s == 1:
                    x_lo(7)
                o, j = t - 3, 2 * ((s - 3) % 4)
                if not (first and t < 3):
                    add_out(2 * o, j)
                probs_lo(t - 1)
                v_piece_lo(t + 1, (s + 1) % 4)
                if not (first and t < 3):
                    add_out(2 * o + 1, j + 1)

            chained = [0]

            def tick(ins):
                chained[0] += 1
                ins.then_inc(f_chain, 1)
                dve.wait_ge(f_chain, chained[0])

            def x_plus_gated(j):
                dve.wait_ge(acc_done, 2 * UNITS - 2 * B + j + 1)
                if j % BH == 0:
                    dve.wait_ge(ld_x2[j // BH], 16)
                    dve.wait_ge(tanh_done, 1)
                dve.scalar_tensor_tensor(out=acc[:, j, :], in0=acc[:, j, :], scalar=tgate[:, 0:1],
                                         in1=x_again[:, j % BH, :], op0=ALU.mult, op1=ALU.add).then_inc(f_u, 1)

            def x1(j):
                n = 2 * UNITS - B + j
                dve.wait_ge(o_done, n + 1)
                dve.wait_ge(f_u, j + 1)
                dve.scalar_tensor_tensor(out=acc[:, j, :], in0=late_bank[n], scalar=tgate[:, 0:1],
                                         in1=acc[:, j, :], op0=ALU.mult, op1=ALU.add).then_inc(f_x1, 1)

            def x1_spread(j):
                dve.wait_ge(f_x1, j + 1)
                dve.bn_stats(bn6[:, j // BH, j % BH, :], acc[:, j, :]).then_inc(f_bn, 1)

            def x1_stats(j):
                dve.wait_ge(f_bn, j + 1)
                dve.bn_aggr(mv[:, j // BH, j % BH, :], bn6[:, j // BH, j % BH, :]).then_inc(f_mv, 1)

            def x1_tile(j):
                x1(j)
                x1_spread(j)

            def x1_pair_stats(r):
                x1_stats(2 * r)
                x1_stats(2 * r + 1)
                dve.wait_ge(f_mv, 2 * r + 2)
                h, pair = r // 2, slice(2 * (r % 2), 2 * (r % 2) + 2)
                dve.tensor_scalar(rstd_in[:, h, pair], mv[:, h, pair, 1], LN_EPS, None, ALU.add).then_inc(f_stat, 1)

            def y(j):
                h, i = j // BH, j % BH
                if i % 2 == 0:
                    dve.wait_ge(f_rstd, j // 2 + 1)
                if j == 0:
                    dve.wait_ge(f_w_lo, 1)
                reached(dve, f_yt, j - 1)
                dve.tensor_scalar(y_ring[j % 2], acc[:, j, :], mv[:, h, i, 0:1], rstd[:, h, i:i + 1],
                                  ALU.subtract, ALU.mult).then_inc(f_y, 1)

            def y_lo(j):
                dve.wait_ge(f_yhi, j + 1)
                low(xT_lo[:, :, tok(j)], yT_bank[j % 2].rearrange("p (c n) -> p c n", c=DC),
                    xT_hi[:, :, tok(j)], f_ylo)

            def router_constants():
                dve.wait_ge(ld_small, 32)
                dve.wait_ge(consts_done, 2)
                tick(dve.tensor_copy(emap_f[:, :], emap[:, :]))
                tick(dve.tensor_copy(eidx_f[:, :], eidx[:, :]))
                for e in range(E):
                    ins = dve.tensor_scalar(onehot[:, e, :], emap_f[:, :], eidx_f[:, e:e + 1], LORA_SCALE,
                                            ALU.is_equal, ALU.mult)
                tick(ins)

            def gated_base_b():
                dve.wait_ge(ld_bb, 16)
                dve.wait_ge(tanh_done, 1)
                dve.tensor_scalar(row_bc[:, :], row_bc[:, :], tgate[:, 1:2], None, ALU.mult).then_inc(f_tb, 1)

            def logits(h):
                for k in range(2):
                    dve.wait_ge(f_rl, 2 * h + k + 1)
                    bc = rb_bc[:, :].rearrange("p (a n) -> p a n", a=1).broadcast_to([P, 2, NR])
                    tick(dve.tensor_tensor(lg[:, 2 * k:2 * k + 2, :], RL[k][:, :, ER:ER + NR], bc, ALU.add))
                tick(dve.tensor_reduce(lmax[:, :], lg[:, :, :], AX.X, ALU.max))
                top = lmax[:, :].rearrange("p (b o) -> p b o", o=1).broadcast_to([P, BH, NR])
                dve.tensor_tensor(lg[:, :, :], lg[:, :, :], top, ALU.subtract).then_inc(f_lg, 1)

            def route(h):
                dve.wait_ge(f_exp, h + 1)
                tick(dve.tensor_reduce(lsum[:, :], le[:, :, :], AX.X, ALU.add))
                tick(dve.reciprocal(lrec[:, :], lsum[:, :]))
                inv = lrec[:, :].rearrange("p (b o) -> p b o", o=1).broadcast_to([P, BH, NR])
                tick(dve.tensor_tensor(probs[:, :, :], le[:, :, :], inv, ALU.mult))
                for i in range(BH):
                    ins = dve.max(top8[:, i, :], probs[:, i, :])
                tick(ins)
                for i in range(BH):
                    ins = dve.match_replace(rest[:, i, :], top8[:, i, :], probs[:, i, :], 0.0)
                tick(ins)
                tick(dve.tensor_tensor(chosen[:, :, :], probs[:, :, :], rest[:, :, :], ALU.subtract))
                sel = chosen[:, :, :].rearrange("p i (a n) -> p i a n", a=1).broadcast_to([P, BH, E, NR])
                one = onehot[:, :, :].rearrange("p (a e) n -> p a e n", a=1).broadcast_to([P, BH, E, NR])
                tick(dve.tensor_tensor(picked[:, :, :, :], sel, one, ALU.mult))
                tick(dve.tensor_reduce(we[:, :, :], picked[:, :, :, :], AX.X, ALU.add))
                reached(dve, f_hwt, h)
                dve.wait_ge(pt_done, UNITS)
                for i in range(BH):
                    w = we[:, i, :].rearrange("p (e o) -> p e o", o=1).broadcast_to([P, E, R])
                    ins = dve.tensor_tensor(hw[:, i, :].rearrange("p (e r) -> p e r", e=E),
                                            RL[i // 2][:, i % 2, 0:ER].rearrange("p (e r) -> p e r", e=E), w, ALU.mult)
                ins.then_inc(f_hw, 1)

            def hw_lo(h):
                dve.wait_ge(f_hwhi, h + 1)
                low(hwT_lo[:, :], Kb[:, :], hwT_hi[:, :], f_hwlo)

            def result(j):
                dve.wait_ge(f_base, j + 1)
                dve.wait_ge(f_x1b, j + 1)
                reached(dve, stored[j % 2], 16 * (j // 2))
                dve.scalar_tensor_tensor(out=out_ring[j % 2], in0=base_bank[j % BH], scalar=tgate[:, 1:2],
                                         in1=x1b[j % 2], op0=ALU.mult, op1=ALU.add).then_inc(f_out, 1)

            for c in range(DC):
                context_lo(0, c)
            layernorm_stats(0)
            mask_valid()
            rms_stats(0)
            mask_negative()
            norm_scales(0)
            v_piece_lo(0, 0)
            for j in range(BH):
                normed(j)
            v_piece_lo(1, 1)
            for j in range(BH):
                x_lo(j)
            k_lo(0)
            layernorm_stats(1)
            q_lo(0)
            context_lo(1, 2)
            rms_stats(1)
            context_lo(1, 3)
            norm_scales(1)
            for j in range(BH, B):
                normed(j)
            for s in range(1, 4):
                step(0, s)
                if s == 2:
                    gated_base_b()
            router_constants()
            with dve.Fori(1, G - 1) as g:
                for s in range(4):
                    step(g, s)
            for s in range(4):
                step(G - 1, s)
                if s == 1:
                    for j in range(BH):
                        x_plus_gated(j)

            k_lo(UNITS - 1)
            x1_tile(0)
            x1_tile(1)
            x1_pair_stats(0)
            probs_lo(UNITS - 2)
            x1_tile(2)
            y(0)
            y(1)
            x1_tile(3)
            y_lo(0)
            x1_pair_stats(1)
            y_lo(1)
            scores(UNITS - 1)
            y(2)
            y(3)
            attention_lo(UNITS - 2, 1, 0)
            y_lo(2)
            y_lo(3)
            normalise(UNITS - 1, 1)
            for j in range(BH, B):
                x_plus_gated(j)
            logits(0)
            probs_lo(UNITS - 1)
            route(0)
            attention_lo(UNITS - 1, 1, 1)
            hw_lo(0)
            x1_tile(4)
            x1_tile(5)
            x1_pair_stats(2)
            x1_tile(6)
            y(4)
            y(5)
            x1_tile(7)
            x1_pair_stats(3)
            y_lo(4)
            y(6)
            y_lo(5)
            y(7)
            result(0)
            result(1)
            y_lo(6)
            y_lo(7)
            result(2)
            result(3)
            logits(1)
            route(1)
            hw_lo(1)
            for j in range(BH, B):
                result(j)

        @block.tensor
        def _(pe):
            def product(dst, w_hi, w_lo, m_hi, m_lo, start, stop):
                pe.matmul(dst, w_lo, m_hi, start=start, stop=False)
                pe.matmul(dst, w_hi, m_lo, start=False, stop=False)
                return pe.matmul(dst, w_hi, m_hi, start=False, stop=stop)

            def x_transpose(j):
                pe.wait_ge(xn_done, j + 1)
                if j >= BH:
                    pe.wait_ge(x_lo_done, 5 if j == 7 else j - BH + 1)
                for c in range(DC):
                    last = pe.transpose(xT_bank[j][:, c * P:(c + 1) * P], xn_at[j % BH][:, c * P:(c + 1) * P],
                                        ident[:, :])
                last.then_inc(xt_psum, 1)

            def project(bank, p, which, source_hi, source_lo, half, done):
                for c in range(DC):
                    last = product(bank, qk_hi[:, p, which, c, :], qk_lo[:, p, which, c, :],
                                   source_hi[:, c, rows(half)], source_lo[:, c, rows(half)], c == 0, c == DC - 1)
                last.then_inc(done, 1)

            def v_piece(v, g, i):
                in_other = isinstance(v, int) and v == 1
                if not in_other:
                    reached(pe, v_lo_done, v)
                bank = V_bank1 if in_other else Vb[:, :, :]
                if i == 0:
                    pe.wait_ge(wv_lo_done, g + 1)
                for k in range(2):
                    j = 2 * i + k
                    for c in range(DC):
                        last = product(bank[:, k, :], cT_hi[:, c, tok(j)], cT_lo[:, c, tok(j)],
                                       v_hi[:, c, :], v_lo[:, c, :], c == 0, c == DC - 1)
                last.then_inc(v_done, 1)

            def out_tile(n, g, j):
                bank = late_bank.get(n, Ob[:, :]) if isinstance(n, int) else Ob[:, :]
                if isinstance(n, int) and n > 2 * UNITS - B:
                    reached(pe, f_x1, n - 1 - (2 * UNITS - B))
                else:
                    reached(pe, acc_done, n)
                half, b = j // BH, j % BH
                if j == 0:
                    pe.wait_ge(wo_lo_done, g + 1)
                if j % BH == 0:
                    pe.wait_ge(a_lo_done, 4 * g + 2 * half + 2)
                for p in range(2):
                    last = product(bank, A_hi[:, half, p, tok(b)], A_lo[:, half, p, tok(b)],
                                   o_hi[:, p, :], o_lo[:, p, :], p == 0, p == 1)
                last.then_inc(o_done, 1)

            def transpose_probs(u):
                pe.wait_ge(norm_done, u + 1)
                for b in range(BH):
                    last = pe.transpose(QP[:, tok(b)], p_norm[:, b, :], ident[:, :])
                last.then_inc(pt_done, 1)

            def scores(u):
                pe.wait_ge(q_lo_done, u + 1)
                pe.wait_ge(k_lo_done, u + 1)
                reached(pe, s_done, u)
                reached(pe, small_s_done, u)
                for b in range(BH):
                    pe.matmul(Sb[:, b, :, :], Q_hi[:, tok(b)], K_hl[:, b, :, :], start=True, stop=False)
                    last = pe.matmul(Sb[:, b, 0, :], Q_lo[:, tok(b)], K_hl[:, b, 0, :], start=False, stop=True)
                last.then_inc(scores_done, 1)

            def apply_probs(u, half, p, v_pieces):
                pe.wait_ge(p_lo_done, u + 1)
                pe.wait_ge(v_lo_done, v_pieces)
                reached(pe, a_lo_done, u)
                reached(pe, small_a_done, u)
                for b in range(BH):
                    j, cols = BH * half + b, slice(p * DH, (p + 1) * DH)
                    pe.matmul(Ab[:, b, :, :], V_hi[:, j, cols], P_hl[:, b, :, :], start=True, stop=False)
                    last = pe.matmul(Ab[:, b, 0, :], V_lo[:, j, cols], P_hl[:, b, 0, :], start=False, stop=True)
                last.then_inc(pv_done, 1)

            def y_transpose(j):
                pe.wait_ge(f_y, j + 1)
                reached(pe, f_ylo, j - 1)
                if j == 0:
                    pe.wait_ge(p_lo_done, UNITS - 1)
                if j == 1:
                    pe.wait_ge(k_lo_done, UNITS)
                if j == BH:
                    pe.wait_ge(f_x1, B)
                for c in range(DC):
                    last = pe.transpose(yT_bank[j % 2][:, c * P:(c + 1) * P], y_ring[j % 2][:, c * P:(c + 1) * P],
                                        ident[:, :])
                last.then_inc(f_yt, 1)

            def q_of(t, g, s):
                if s < 2:
                    pe.wait_ge(qk_lo_done, 2 * g + s % 2 + 1)
                reached(pe, p_lo_done, t - 1)
                project(QP[:, :], s % 2, 0, xT_hi, xT_lo, s // 2, q_done)

            def k_of(t, g, s):
                if s < 2:
                    pe.wait_ge(qk_lo_done, 2 * g + s % 2 + 1)
                reached(pe, k_lo_done, t)
                project(Kb[:, :], s % 2, 1, cT_hi, cT_lo, s // 2, k_done)

            def step(g, s):
                t = 4 * g + s
                first, last = (isinstance(g, int) and g == n for n in (0, G - 1))
                final = last and s == 3
                if first and s == 1:
                    k_of(t, g, s)
                    scores(0)
                q_of(t, g, s)
                if final:
                    k_of(t, g, s)
                    pe.wait_ge(v_lo_done, UNITS)
                    out_tile(2 * UNITS - 8, g, 0)
                    pe.wait_ge(q_lo_done, t + 1)
                    transpose_probs(t - 1)
                    out_tile(2 * UNITS - 7, g, 1)
                    scores(t)
                    out_tile(2 * UNITS - 6, g, 2)
                    out_tile(2 * UNITS - 5, g, 3)
                    y_transpose(0)
                    y_transpose(1)
                    apply_probs(t - 1, 1, 0, 4 * g + 4)
                    return
                if not (first and s == 1):
                    k_of(t, g, s)
                o, j = t - 3, 2 * ((s - 3) % 4)
                og = g if s == 3 else g - 1
                outs = not (first and t < 3)
                if outs:
                    out_tile(2 * o, og, j)
                if first and s == 1:
                    for n in range(BH, B):
                        x_transpose(n)
                    pe.wait_ge(c_lo_done, 2 * DC)
                v_piece(t + 1, g + (s == 3), (s + 1) % 4)
                pe.wait_ge(q_lo_done, t + 1)
                transpose_probs(t - 1)
                if outs:
                    out_tile(2 * o + 1, og, j + 1)
                scores(t)
                u_half, u_p = ((s - 1) % 4) // 2, (s - 1) % 2
                u_g4 = 4 * (g if s > 0 else g - 1)
                apply_probs(t - 1, u_half, u_p, u_g4 + 2 * u_half + 2)

            pe.wait_ge(c_lo_done, DC)
            v_piece(0, 0, 0)
            v_piece(1, 0, 1)
            pe.wait_ge(ident_done, 1)
            for j in range(BH):
                x_transpose(j)
            k_of(0, 0, 0)
            pe.wait_ge(x_lo_done, BH)
            q_of(0, 0, 0)
            pe.wait_ge(v_lo_done, 2)
            step(0, 1)
            pe.wait_ge(x_lo_done, B)
            step(0, 2)
            step(0, 3)
            with pe.Fori(1, G - 1) as g:
                for s in range(4):
                    step(g, s)
            for s in range(4):
                step(G - 1, s)

            def lora_and_router(h, k):
                pe.wait_ge(f_w_lo, 1)
                reached(pe, f_hw, h)
                if h == 0:
                    pe.wait_ge(f_x1, BH)
                for i in (2 * k, 2 * k + 1):
                    j = BH * h + i
                    pe.wait_ge(f_ylo, j + 1)
                    for c in range(DC):
                        last = product(RL[i // 2][:, i % 2, :], xT_hi[:, c, tok(j)], xT_lo[:, c, tok(j)],
                                       v_hi[:, c, 0:RW], v_lo[:, c, 0:RW], c == 0, c == DC - 1)
                    if i % 2:
                        last.then_inc(f_rl, 1)

            def base(j):
                i = j % BH
                pe.wait_ge(f_w_lo, 3)
                if j == 0:
                    pe.wait_ge(s_done, UNITS)
                    pe.wait_ge(small_s_done, UNITS)
                if j == 2:
                    pe.wait_ge(a_lo_done, UNITS)
                reached(pe, f_out, j - BH + 1)
                for c in range(DC):
                    product(base_bank[i], xT_hi[:, c, tok(j)], xT_lo[:, c, tok(j)],
                            w_base_hi[:, c, :], w_base_lo[:, c, :], c == 0, False)

            def hw_transpose(h):
                pe.wait_ge(f_hw, h + 1)
                pe.wait_ge(f_ylo, BH * (h + 1))
                for i in range(BH):
                    last = pe.transpose(Kb[:, tok(i)], hw[:, i, :], ident[:, :])
                last.then_inc(f_hwt, 1)

            def lora_out(j):
                i = j % BH
                pe.wait_ge(f_hwlo, j // BH + 1)
                pe.wait_ge(f_w_lo, 4)
                product(base_bank[i], hwT_hi[:, tok(i)], hwT_lo[:, tok(i)], w_loraB_hi, w_loraB_lo,
                        False, True).then_inc(f_base, 1)

            lora_and_router(0, 0)
            y_transpose(2)
            y_transpose(3)
            lora_and_router(0, 1)
            pe.wait_ge(f_ylo, BH)
            transpose_probs(UNITS - 1)
            base(0)
            apply_probs(UNITS - 1, 1, 1, UNITS)
            base(1)
            hw_transpose(0)
            pe.wait_ge(p_lo_done, UNITS)
            out_tile(2 * UNITS - 4, G - 1, 4)
            pe.wait_ge(f_hwlo, 1)
            for j in range(5, B):
                out_tile(2 * UNITS - B + j, G - 1, j)
            base(2)
            y_transpose(4)
            y_transpose(5)
            lora_out(0)
            lora_out(1)
            base(3)
            y_transpose(6)
            y_transpose(7)
            lora_out(2)
            lora_out(3)
            lora_and_router(1, 0)
            lora_and_router(1, 1)
            base(4)
            base(5)
            hw_transpose(1)
            base(6)
            lora_out(4)
            lora_out(5)
            base(7)
            lora_out(6)
            lora_out(7)


_INPUTS = ["x", "ctxT", "mask", "g_xattn", "g_ffn", "bias", "lnw", "wqk", "wv", "wo", "baseT", "base_b",
           "loraR", "router_b", "lora_B", "expert_map"]


def kernel(x, ctx_4096, mask_BxSxS2_bk0, g_xattn, g_ffn, L0_xattn_position_bias, L0_xattn_ln_weight,
           L0_xattn_w_q, L0_xattn_w_k, L0_xattn_w_v, L0_xattn_w_out, L0_ffn_base_W, L0_ffn_base_b,
           L0_ffn_router_W, L0_ffn_router_b, L0_ffn_A, L0_ffn_B, L0_ffn_expert_map):
    import numpy as np
    import concourse.bacc as bacc
    from concourse.bass_utils import run_bass_kernel_spmd

    def by_chunk(w):
        return np.asarray(w).reshape(-1, DC, P).transpose(2, 1, 0)

    def heads(w, n):
        return np.asarray(w).reshape(H // n, n * DH, DC, P).transpose(0, 3, 2, 1)

    given = {
        "x": np.asarray(x).transpose(1, 0, 2),
        "ctxT": by_chunk(np.asarray(ctx_4096).reshape(B * S, D)),
        "mask": np.asarray(mask_BxSxS2_bk0).transpose(1, 0, 2),
        "g_xattn": np.asarray(g_xattn).reshape(1, 1),
        "g_ffn": np.asarray(g_ffn).reshape(1, 1),
        "bias": np.asarray(L0_xattn_position_bias),
        "lnw": np.asarray(L0_xattn_ln_weight).reshape(1, D),
        "wqk": np.stack([heads(L0_xattn_w_q, 1), heads(L0_xattn_w_k, 1)], axis=2),
        "wv": heads(L0_xattn_w_v, 2),
        "wo": np.asarray(L0_xattn_w_out).reshape(D, G, 2, DH).transpose(1, 3, 2, 0),
        "baseT": by_chunk(L0_ffn_base_W),
        "base_b": np.asarray(L0_ffn_base_b).reshape(1, D),
        "loraR": np.concatenate([by_chunk(np.asarray(L0_ffn_A).reshape(ER, D)), by_chunk(L0_ffn_router_W),
                                 np.zeros((P, DC, 1), np.float32)], axis=2),
        "router_b": np.asarray(L0_ffn_router_b).reshape(1, NR),
        "lora_B": np.asarray(L0_ffn_B).transpose(0, 2, 1).reshape(ER, D),
        "expert_map": np.asarray(L0_ffn_expert_map).reshape(1, NR),
    }
    given = {name: np.ascontiguousarray(a) for name, a in given.items()}

    nc = bacc.Bacc("TRN2", target_bir_lowering=False, num_devices=1)
    args = [nc.dram_tensor(n, given[n].shape, mybir.dt.from_np(given[n].dtype), kind="ExternalInput").ap()
            for n in _INPUTS]
    args.append(nc.dram_tensor("out", (P, B, D), F32, kind="ExternalOutput").ap())
    build(nc, *args)
    result = run_bass_kernel_spmd(nc, [given], core_ids=[0]).results[0]["out"]
    return result.transpose(1, 0, 2)
```
